# Optimizing a Trainium2 kernel written in Bass

```python
import numpy as np
import jax
import jax.numpy as jnp

def _softmax(x, axis=-1):
    return jax.nn.softmax(x, axis=axis)

def _gelu(x):
    return jax.nn.gelu(x, approximate=True)

def _silu(x):
    return jax.nn.silu(x)

def _sigmoid(x):
    return jax.nn.sigmoid(x)

def _layernorm(x, axis=-1, eps=1e-05):
    m = jnp.mean(x, axis=axis, keepdims=True)
    v = jnp.var(x, axis=axis, keepdims=True)
    return (x - m) / jnp.sqrt(v + eps)

def _scatter_add(tgt, idx, src, axis=0):
    return tgt.at[idx].add(src)

def _segment_sum(src, seg, n):
    return jax.ops.segment_sum(src, seg, n)
kernel_name = 'mk_flamingo_gated_d4_seqx_r8_e8928a'

def setup_inputs(seed: int=0):
    np.random.seed(seed)
    _w = jnp.asarray

    def _rec_inputs():
        import jax
        import jax.numpy as jnp
        _rk = jax.random.key(seed)
        x = -0.0002928 + 1 * jax.random.normal(jax.random.fold_in(_rk, 1), (32, 100, 128), jnp.float32)
        _lenS = 100 - jax.random.randint(jax.random.fold_in(_rk, 7), (32,), 0, max(1, 100 // 4) + 1, jnp.int32)
        _lenS2 = 1444 - jax.random.randint(jax.random.fold_in(_rk, 8), (32,), 0, max(1, 1444 // 4) + 1, jnp.int32)
        _ctx_1024P = jax.random.normal(jax.random.fold_in(_rk, 11), (32, 16, 128), jnp.float32)
        _ctx_1024c = jax.random.dirichlet(jax.random.fold_in(_rk, 511), 0.3 * jnp.ones((16,), jnp.float32), (32, 1444))
        _ctx_1024t = jnp.einsum('bsk,bkd->bsd', _ctx_1024c, _ctx_1024P)
        _ctx_1024t = _ctx_1024t * jax.lax.rsqrt(jnp.mean(jnp.square(_ctx_1024t)) + 1e-12) * 0.953939
        ctx_1024 = -1.39393e-06 + 0.999914 * (_ctx_1024t + 0.3 * jax.random.normal(jax.random.fold_in(_rk, 611), (32, 1444, 128), jnp.float32))
        _validS = jnp.arange(100)[None, :] < _lenS[:, None]
        _validS2 = jnp.arange(1444)[None, :] < _lenS2[:, None]
        _causal = jnp.tril(jnp.ones((100, 100), dtype=bool))
        mask_Bx1xSxS2_ik1 = jnp.where(jnp.broadcast_to(_validS2[:, None, None, :], (32, 1, 100, 1444)), 1, 0).astype(jnp.int32)
        mask_BxSxS2_ik1 = jnp.where(jnp.broadcast_to(_validS2[:, None, :], (32, 100, 1444)), 1, 0).astype(jnp.int32)
        mask_B_ik0 = jnp.where(jnp.ones((32,), dtype=bool), 69, 1564).astype(jnp.int32)
        _g = jax.random.normal(jax.random.fold_in(_rk, 9001), (2, 4), jnp.float32)
        _g = jnp.sign(_g) * jnp.maximum(jnp.abs(_g), 1.0) + (_g == 0) * 1.0
        g_xattn = _g[0]
        g_ffn = _g[1]
        return (x, ctx_1024, mask_Bx1xSxS2_ik1, mask_BxSxS2_ik1, mask_B_ik0, g_xattn, g_ffn)
    x, ctx_1024, mask_Bx1xSxS2_ik1, mask_BxSxS2_ik1, mask_B_ik0, g_xattn, g_ffn = _rec_inputs()

    def _L0_xattn_setup():
        import jax, jax.numpy as jnp
        import numpy as np
        D_MODEL = 128
        HEADS = 16
        D_K = D_MODEL // HEADS
        B, S = (2, 256)
        key = jax.random.key(seed)
        ks = jax.random.split(key, 11)
        sc = 1.0 / np.sqrt(D_MODEL)
        return {'q': jax.random.normal(ks[0], (B, S, D_MODEL), jnp.float32), 'k': jax.random.normal(ks[1], (B, S, D_MODEL), jnp.float32), 'v': jax.random.normal(ks[2], (B, S, D_MODEL), jnp.float32), 'Wq': jax.random.normal(ks[3], (D_MODEL, D_MODEL), jnp.float32) * sc, 'bq': jnp.zeros((D_MODEL,), jnp.float32), 'Wk': jax.random.normal(ks[4], (D_MODEL, D_MODEL), jnp.float32) * sc, 'bk': jnp.zeros((D_MODEL,), jnp.float32), 'Wv': jax.random.normal(ks[5], (D_MODEL, D_MODEL), jnp.float32) * sc, 'bv': jnp.zeros((D_MODEL,), jnp.float32), 'Wo': jax.random.normal(ks[6], (D_MODEL, D_MODEL), jnp.float32) * sc, 'bo': jnp.zeros((D_MODEL,), jnp.float32)}
    _L0_xattn_all = _L0_xattn_setup()
    _L0_xattn_in = {k: v for k, v in _L0_xattn_all.items() if k in ('Wq', 'bq', 'Wk', 'bk', 'Wv', 'bv', 'Wo', 'bo')}
    del _L0_xattn_all

    def _L0_ffn_setup():
        import jax, jax.numpy as jnp
        import numpy as np
        B, S, H = (4, 256, 128)
        E, K = (8, 2)
        I_R, I_S = (4 * H, 8 * H)
        CAP_FACTOR = 1.25
        SCALE = 1.0
        key = jax.random.key(seed)
        ks = jax.random.split(key, 9)
        std = 0.02
        return {'x': jax.random.normal(ks[0], (B, S, H), jnp.float32), 'router_w': std * jax.random.normal(ks[1], (E, H), jnp.float32), 'rg': std * jax.random.normal(ks[2], (E, H, I_R), jnp.float32), 'ru': std * jax.random.normal(ks[3], (E, H, I_R), jnp.float32), 'rd': std * jax.random.normal(ks[4], (E, I_R, H), jnp.float32), 'sg': std * jax.random.normal(ks[5], (H, I_S), jnp.float32), 'su': std * jax.random.normal(ks[6], (H, I_S), jnp.float32), 'sd': std * jax.random.normal(ks[7], (I_S, H), jnp.float32)}
    _L0_ffn_all = _L0_ffn_setup()
    _L0_ffn_in = {k: v for k, v in _L0_ffn_all.items() if k in ('router_w', 'rg', 'ru', 'rd', 'sg', 'su', 'sd')}
    del _L0_ffn_all

    def _L1_xattn_setup():
        import jax, jax.numpy as jnp
        import numpy as np
        NUM_HEADS = 16
        INPUT_SIZE = 128
        HEAD_SIZE = INPUT_SIZE // NUM_HEADS
        B, L = (4, 256)
        key = jax.random.key(seed)
        ks = jax.random.split(key, 6)
        keys = jax.random.normal(ks[0], (B, L, INPUT_SIZE), dtype=jnp.float32)
        values = jax.random.normal(ks[1], (B, L, INPUT_SIZE), dtype=jnp.float32)
        queries = jax.random.normal(ks[2], (B, L, INPUT_SIZE), dtype=jnp.float32)
        mask = jax.random.randint(ks[3], (B, 1, L, L), 0, 2, dtype=jnp.int32)
        W_v = jax.random.normal(ks[4], (HEAD_SIZE, HEAD_SIZE), dtype=jnp.float32) / np.sqrt(HEAD_SIZE)
        W_o = jax.random.normal(ks[5], (INPUT_SIZE, INPUT_SIZE), dtype=jnp.float32) / np.sqrt(INPUT_SIZE)
        return {'keys': keys, 'values': values, 'queries': queries, 'mask': mask, 'W_v': W_v, 'W_o': W_o}
    _L1_xattn_all = _L1_xattn_setup()
    _L1_xattn_in = {k: v for k, v in _L1_xattn_all.items() if k in ('W_v', 'W_o')}
    del _L1_xattn_all

    def _L1_ffn_setup():
        import jax, jax.numpy as jnp
        import numpy as np
        DIM = 128
        INTER = 64
        E = 32
        TOPK = 4
        GROUPS = 8
        TOPK_GROUPS = 4
        SHARED_INTER = 2 * INTER
        ROUTE_SCALE = 1.0
        B, S = (8, 512)

        def _gate(xf, gw, gb):
            T = xf.shape[0]
            scores = jax.nn.softmax((xf @ gw + gb).astype(jnp.float32), axis=-1)
            original_scores = scores
            scores_g = scores.reshape(T, GROUPS, E // GROUPS)
            group_scores = jnp.sum(jax.lax.top_k(scores_g, 2)[0], axis=-1)
            gidx = jax.lax.top_k(group_scores, TOPK_GROUPS)[1]
            keep = jnp.zeros((T, GROUPS), bool).at[jnp.arange(T)[:, None], gidx].set(True)
            masked = jnp.where(keep[:, :, None], scores_g, -jnp.inf).reshape(T, E)
            indices = jax.lax.top_k(masked, TOPK)[1]
            weights = jnp.take_along_axis(original_scores, indices, axis=1) * ROUTE_SCALE
            return (weights.astype(xf.dtype), indices)
        key = jax.random.key(seed)
        ks = jax.random.split(key, 16)

        def xav(k, shape):
            fan_in, fan_out = (shape[-2], shape[-1])
            lim = np.sqrt(6.0 / (fan_in + fan_out))
            return jax.random.uniform(k, shape, jnp.float32, -lim, lim)
        return {'x': jax.random.normal(ks[0], (B, S, DIM), jnp.float32), 'gw': xav(ks[1], (DIM, E)), 'gb': jnp.zeros((E,), jnp.float32), 'w1': xav(ks[2], (E, DIM, INTER)), 'b1': jnp.zeros((E, INTER), jnp.float32), 'w3': xav(ks[3], (E, DIM, INTER)), 'b3': jnp.zeros((E, INTER), jnp.float32), 'w2': xav(ks[4], (E, INTER, DIM)), 'b2': jnp.zeros((E, DIM), jnp.float32), 'sw1': xav(ks[5], (DIM, SHARED_INTER)), 'sb1': jnp.zeros((SHARED_INTER,), jnp.float32), 'sw3': xav(ks[6], (DIM, SHARED_INTER)), 'sb3': jnp.zeros((SHARED_INTER,), jnp.float32), 'sw2': xav(ks[7], (SHARED_INTER, DIM)), 'sb2': jnp.zeros((DIM,), jnp.float32)}
    _L1_ffn_all = _L1_ffn_setup()
    _L1_ffn_in = {k: v for k, v in _L1_ffn_all.items() if k in ('gw', 'gb', 'w1', 'b1', 'w3', 'b3', 'w2', 'b2', 'sw1', 'sb1', 'sw3', 'sb3', 'sw2', 'sb2')}
    del _L1_ffn_all

    def _L2_xattn_setup():
        import jax, jax.numpy as jnp
        import numpy as np
        B, L, H = (8, 256, 128)
        SCALE = float(np.sqrt(H))
        EPS = 1e-05
        key = jax.random.key(seed)
        ks = jax.random.split(key, 12)
        s = 1.0 / np.sqrt(H)
        return {'queries': jax.random.normal(ks[0], (B, L, H), jnp.float32), 'keys': jax.random.normal(ks[1], (B, L, H), jnp.float32), 'values': jax.random.normal(ks[2], (B, L, H), jnp.float32), 'mask': jax.random.randint(ks[3], (B, L, L), 0, 2, jnp.int32), 'Wq': jax.random.normal(ks[4], (H, H), jnp.float32) * s, 'bq': jnp.zeros((H,), jnp.float32), 'Wk': jax.random.normal(ks[5], (H, H), jnp.float32) * s, 'bk': jnp.zeros((H,), jnp.float32), 'Wv': jax.random.normal(ks[6], (H, H), jnp.float32) * s, 'bv': jnp.zeros((H,), jnp.float32), 'ln_gamma': jnp.ones((H,), jnp.float32), 'ln_beta': jnp.zeros((H,), jnp.float32)}
    _L2_xattn_all = _L2_xattn_setup()
    _L2_xattn_in = {k: v for k, v in _L2_xattn_all.items() if k in ('Wq', 'bq', 'Wk', 'bk', 'Wv', 'bv', 'ln_gamma', 'ln_beta')}
    del _L2_xattn_all

    def _L2_ffn_setup():
        import jax, jax.numpy as jnp
        import numpy as np
        S, B, H, I, E = (64, 2, 128, 352, 8)
        key = jax.random.key(seed)
        ks = jax.random.split(key, 5)
        return {'hidden_states': jax.random.normal(ks[0], (S, B, H), dtype=jnp.float32), 'router_w': jax.random.normal(ks[1], (E, H), dtype=jnp.float32) * 0.02, 'gate_w': jax.random.normal(ks[2], (E, I, H), dtype=jnp.float32) * 0.02, 'up_w': jax.random.normal(ks[3], (E, I, H), dtype=jnp.float32) * 0.02, 'down_w': jax.random.normal(ks[4], (E, H, I), dtype=jnp.float32) * 0.02}
    _L2_ffn_all = _L2_ffn_setup()
    _L2_ffn_in = {k: v for k, v in _L2_ffn_all.items() if k in ('router_w', 'gate_w', 'up_w', 'down_w')}
    del _L2_ffn_all

    def _L3_xattn_setup():
        import jax, jax.numpy as jnp
        import numpy as np
        import math
        B, S, D, H = (2, 256, 128, 16)
        DH = D // H
        MASK_VALUE = -1000000.0

        def _split_heads(x):
            b, s, d = x.shape
            return x.reshape(b, s, H, DH).transpose(0, 2, 1, 3)
        key = jax.random.key(seed)
        ks = jax.random.split(key, 8)
        scale = 1.0 / math.sqrt(D)
        return {'queries': jax.random.normal(ks[0], (B, S, D), jnp.float32), 'keys': jax.random.normal(ks[1], (B, S, D), jnp.float32), 'values': jax.random.normal(ks[2], (B, S, D), jnp.float32), 'valid_lens': jax.random.randint(ks[3], (B,), 1, S + 1, jnp.int32), 'Wq': jax.random.normal(ks[4], (D, D), jnp.float32) * scale, 'Wk': jax.random.normal(ks[5], (D, D), jnp.float32) * scale, 'Wv': jax.random.normal(ks[6], (D, D), jnp.float32) * scale, 'Wo': jax.random.normal(ks[7], (D, D), jnp.float32) * scale}
    _L3_xattn_all = _L3_xattn_setup()
    _L3_xattn_in = {k: v for k, v in _L3_xattn_all.items() if k in ('Wq', 'Wk', 'Wv', 'Wo')}
    del _L3_xattn_all

    def _L3_ffn_setup():
        import jax, jax.numpy as jnp
        import numpy as np
        DIM = 128

        def _reference_tuple_inner(x, W_r, W_k, W_v, mu_r, mu_k):
            B, T, C = x.shape
            x_prev = jnp.concatenate([jnp.zeros((B, 1, C), x.dtype), x[:, :-1, :]], axis=1)
            xr = mu_r * x + (1.0 - mu_r) * x_prev
            xk = mu_k * x + (1.0 - mu_k) * x_prev
            r = jax.nn.sigmoid(jnp.einsum('btc,dc->btd', xr, W_r))
            k = jnp.einsum('btc,dc->btd', xk, W_k)
            k_act = jnp.square(jax.nn.relu(k))
            out = r * jnp.einsum('btc,dc->btd', k_act, W_v)
            new_state = x[:, -1, :]
            return (out, new_state)
        key = jax.random.key(seed)
        ks = jax.random.split(key, 6)
        B, T, C = (8, 256, DIM)
        x = jax.random.normal(ks[0], (B, T, C), dtype=jnp.float32)
        s = 1.0 / np.sqrt(C)
        W_r = jax.random.uniform(ks[1], (C, C), jnp.float32, -s, s)
        W_k = jax.random.uniform(ks[2], (C, C), jnp.float32, -s, s)
        W_v = jax.random.uniform(ks[3], (C, C), jnp.float32, -s, s)
        mu_r = jax.random.uniform(ks[4], (C,), jnp.float32)
        mu_k = jax.random.uniform(ks[5], (C,), jnp.float32)
        return {'x': x, 'W_r': W_r, 'W_k': W_k, 'W_v': W_v, 'mu_r': mu_r, 'mu_k': mu_k}
    _L3_ffn_all = _L3_ffn_setup()
    _L3_ffn_in = {k: v for k, v in _L3_ffn_all.items() if k in ('W_r', 'W_k', 'W_v', 'mu_r', 'mu_k')}
    del _L3_ffn_all
    return {'x': x, 'ctx_1024': ctx_1024, 'mask_Bx1xSxS2_ik1': mask_Bx1xSxS2_ik1, 'mask_BxSxS2_ik1': mask_BxSxS2_ik1, 'mask_B_ik0': mask_B_ik0, 'g_xattn': g_xattn, 'g_ffn': g_ffn, 'L0_xattn_Wq': _L0_xattn_in['Wq'], 'L0_xattn_bq': _L0_xattn_in['bq'], 'L0_xattn_Wk': _L0_xattn_in['Wk'], 'L0_xattn_bk': _L0_xattn_in['bk'], 'L0_xattn_Wv': _L0_xattn_in['Wv'], 'L0_xattn_bv': _L0_xattn_in['bv'], 'L0_xattn_Wo': _L0_xattn_in['Wo'], 'L0_xattn_bo': _L0_xattn_in['bo'], 'L0_ffn_router_w': _L0_ffn_in['router_w'], 'L0_ffn_rg': _L0_ffn_in['rg'], 'L0_ffn_ru': _L0_ffn_in['ru'], 'L0_ffn_rd': _L0_ffn_in['rd'], 'L0_ffn_sg': _L0_ffn_in['sg'], 'L0_ffn_su': _L0_ffn_in['su'], 'L0_ffn_sd': _L0_ffn_in['sd'], 'L1_xattn_W_v': _L1_xattn_in['W_v'], 'L1_xattn_W_o': _L1_xattn_in['W_o'], 'L1_ffn_gw': _L1_ffn_in['gw'], 'L1_ffn_gb': _L1_ffn_in['gb'], 'L1_ffn_w1': _L1_ffn_in['w1'], 'L1_ffn_b1': _L1_ffn_in['b1'], 'L1_ffn_w3': _L1_ffn_in['w3'], 'L1_ffn_b3': _L1_ffn_in['b3'], 'L1_ffn_w2': _L1_ffn_in['w2'], 'L1_ffn_b2': _L1_ffn_in['b2'], 'L1_ffn_sw1': _L1_ffn_in['sw1'], 'L1_ffn_sb1': _L1_ffn_in['sb1'], 'L1_ffn_sw3': _L1_ffn_in['sw3'], 'L1_ffn_sb3': _L1_ffn_in['sb3'], 'L1_ffn_sw2': _L1_ffn_in['sw2'], 'L1_ffn_sb2': _L1_ffn_in['sb2'], 'L2_xattn_Wq': _L2_xattn_in['Wq'], 'L2_xattn_bq': _L2_xattn_in['bq'], 'L2_xattn_Wk': _L2_xattn_in['Wk'], 'L2_xattn_bk': _L2_xattn_in['bk'], 'L2_xattn_Wv': _L2_xattn_in['Wv'], 'L2_xattn_bv': _L2_xattn_in['bv'], 'L2_xattn_ln_gamma': _L2_xattn_in['ln_gamma'], 'L2_xattn_ln_beta': _L2_xattn_in['ln_beta'], 'L2_ffn_router_w': _L2_ffn_in['router_w'], 'L2_ffn_gate_w': _L2_ffn_in['gate_w'], 'L2_ffn_up_w': _L2_ffn_in['up_w'], 'L2_ffn_down_w': _L2_ffn_in['down_w'], 'L3_xattn_Wq': _L3_xattn_in['Wq'], 'L3_xattn_Wk': _L3_xattn_in['Wk'], 'L3_xattn_Wv': _L3_xattn_in['Wv'], 'L3_xattn_Wo': _L3_xattn_in['Wo'], 'L3_ffn_W_r': _L3_ffn_in['W_r'], 'L3_ffn_W_k': _L3_ffn_in['W_k'], 'L3_ffn_W_v': _L3_ffn_in['W_v'], 'L3_ffn_mu_r': _L3_ffn_in['mu_r'], 'L3_ffn_mu_k': _L3_ffn_in['mu_k']}

def reference(x, ctx_1024, mask_Bx1xSxS2_ik1, mask_BxSxS2_ik1, mask_B_ik0, g_xattn, g_ffn, L0_xattn_Wq, L0_xattn_bq, L0_xattn_Wk, L0_xattn_bk, L0_xattn_Wv, L0_xattn_bv, L0_xattn_Wo, L0_xattn_bo, L0_ffn_router_w, L0_ffn_rg, L0_ffn_ru, L0_ffn_rd, L0_ffn_sg, L0_ffn_su, L0_ffn_sd, L1_xattn_W_v, L1_xattn_W_o, L1_ffn_gw, L1_ffn_gb, L1_ffn_w1, L1_ffn_b1, L1_ffn_w3, L1_ffn_b3, L1_ffn_w2, L1_ffn_b2, L1_ffn_sw1, L1_ffn_sb1, L1_ffn_sw3, L1_ffn_sb3, L1_ffn_sw2, L1_ffn_sb2, L2_xattn_Wq, L2_xattn_bq, L2_xattn_Wk, L2_xattn_bk, L2_xattn_Wv, L2_xattn_bv, L2_xattn_ln_gamma, L2_xattn_ln_beta, L2_ffn_router_w, L2_ffn_gate_w, L2_ffn_up_w, L2_ffn_down_w, L3_xattn_Wq, L3_xattn_Wk, L3_xattn_Wv, L3_xattn_Wo, L3_ffn_W_r, L3_ffn_W_k, L3_ffn_W_v, L3_ffn_mu_r, L3_ffn_mu_k):
    import jax
    import jax.numpy as jnp

    def _L0_xattn_ref(q, k, v, Wq, bq, Wk, bk, Wv, bv, Wo, bo):
        import jax, jax.numpy as jnp
        import numpy as np
        D_MODEL = 128
        HEADS = 16
        D_K = D_MODEL // HEADS
        B, S = (2, 256)
        bs = q.shape[0]

        def proj(x, W, b):
            y = x @ W.T + b
            return y.reshape(bs, -1, HEADS, D_K).transpose(0, 2, 1, 3)
        qh = proj(q, Wq, bq)
        kh = proj(k, Wk, bk)
        vh = proj(v, Wv, bv)
        scores = jnp.einsum('bhqd,bhkd->bhqk', qh, kh) / jnp.sqrt(jnp.asarray(D_K, jnp.float32))
        attn = jax.nn.softmax(scores, axis=-1)
        out = jnp.einsum('bhqk,bhkd->bhqd', attn, vh)
        concat = out.transpose(0, 2, 1, 3).reshape(bs, -1, D_MODEL)
        return concat @ Wo.T + bo

    def _L0_ffn_ref(x, router_w, rg, ru, rd, sg, su, sd):
        import jax, jax.numpy as jnp
        import numpy as np
        B, S, H = (4, 256, 128)
        E, K = (8, 2)
        I_R, I_S = (4 * H, 8 * H)
        CAP_FACTOR = 1.25
        SCALE = 1.0
        b, s, h = x.shape
        T = b * s
        capacity = max(int(CAP_FACTOR * T / E), 1)
        xf = x.reshape(T, h)
        eps = jnp.finfo(x.dtype).eps
        xn = xf * jax.lax.rsqrt(jnp.mean(xf * xf, axis=-1, keepdims=True) + eps)
        logits = xn @ router_w.T
        probs = jax.nn.softmax(logits, axis=-1)
        topk_p, topk_i = jax.lax.top_k(probs, K)
        rw = topk_p / jnp.sum(topk_p, axis=-1, keepdims=True)
        one_hot = jax.nn.one_hot(topk_i, E, dtype=x.dtype)
        mask = one_hot.sum(1)
        wdense = (one_hot * rw[..., None]).sum(1)
        sel = mask.T.astype(bool)
        order = jnp.argsort(~sel, axis=1, stable=True)
        dispatch = order[:, :capacity]
        count = sel.sum(axis=1)
        valid = (jnp.arange(capacity)[None, :] < count[:, None]).astype(x.dtype)
        xg = xf[dispatch]
        gate = jax.nn.silu(jnp.einsum('ech,ehi->eci', xg, rg))
        up = jnp.einsum('ech,ehi->eci', xg, ru)
        eout = jnp.einsum('eci,eih->ech', gate * up, rd)
        w = jnp.take_along_axis(wdense.T, dispatch, axis=1)
        contrib = eout * (w * valid)[..., None]
        routed = jnp.zeros_like(xf).at[dispatch.reshape(-1)].add(contrib.reshape(-1, h))
        shared = jax.nn.silu(x @ sg) * (x @ su) @ sd
        return shared + SCALE * routed.reshape(b, s, h)

    def _L1_xattn_ref(keys, values, queries, mask, W_v, W_o):
        import jax, jax.numpy as jnp
        import numpy as np
        NUM_HEADS = 16
        INPUT_SIZE = 128
        HEAD_SIZE = INPUT_SIZE // NUM_HEADS
        B, L = (4, 256)
        b, q_len, d = queries.shape
        k_len = keys.shape[1]
        n, h = (NUM_HEADS, HEAD_SIZE)
        k = jnp.einsum('bknh,oh->bkno', keys.reshape(b, k_len, n, h), W_v)
        v = jnp.einsum('bknh,oh->bkno', values.reshape(b, k_len, n, h), W_v)
        q = jnp.einsum('bqnh,oh->bqno', queries.reshape(b, q_len, n, h), W_v)
        z = jnp.einsum('bqnh,bknh->bnqk', q, k)
        z = jnp.where(mask == 0, jnp.float32(-1e-20), z)
        attention = jax.nn.softmax(z / jnp.sqrt(jnp.float32(d)), axis=3)
        out = jnp.einsum('bnqk,bknh->bqnh', attention, v).reshape(b, q_len, n * h)
        out = jnp.einsum('bqd,od->bqo', out, W_o)
        return out

    def _L1_ffn_ref(x, gw, gb, w1, b1, w3, b3, w2, b2, sw1, sb1, sw3, sb3, sw2, sb2):
        import jax, jax.numpy as jnp
        import numpy as np
        DIM = 128
        INTER = 64
        E = 32
        TOPK = 4
        GROUPS = 8
        TOPK_GROUPS = 4
        SHARED_INTER = 2 * INTER
        ROUTE_SCALE = 1.0
        B, S = (8, 512)

        def _gate(xf, gw, gb):
            T = xf.shape[0]
            scores = jax.nn.softmax((xf @ gw + gb).astype(jnp.float32), axis=-1)
            original_scores = scores
            scores_g = scores.reshape(T, GROUPS, E // GROUPS)
            group_scores = jnp.sum(jax.lax.top_k(scores_g, 2)[0], axis=-1)
            gidx = jax.lax.top_k(group_scores, TOPK_GROUPS)[1]
            keep = jnp.zeros((T, GROUPS), bool).at[jnp.arange(T)[:, None], gidx].set(True)
            masked = jnp.where(keep[:, :, None], scores_g, -jnp.inf).reshape(T, E)
            indices = jax.lax.top_k(masked, TOPK)[1]
            weights = jnp.take_along_axis(original_scores, indices, axis=1) * ROUTE_SCALE
            return (weights.astype(xf.dtype), indices)
        shape = x.shape
        xf = x.reshape(-1, DIM)
        T = xf.shape[0]
        weights, indices = _gate(xf, gw, gb)
        cw = jnp.zeros((T, E), xf.dtype).at[jnp.arange(T)[:, None], indices].add(weights)

        def body(y, p):
            w1e, b1e, w3e, b3e, w2e, b2e, we = p
            h = jax.nn.silu(xf @ w1e + b1e) * (xf @ w3e + b3e)
            return (y + we[:, None] * (h @ w2e + b2e), None)
        y0 = jnp.zeros_like(xf)
        y, _ = jax.lax.scan(body, y0, (w1, b1, w3, b3, w2, b2, cw.T))
        z = jax.nn.silu(xf @ sw1 + sb1) * (xf @ sw3 + sb3) @ sw2 + sb2
        return (y + z).reshape(shape)

    def _L2_xattn_ref(queries, keys, values, mask, Wq, bq, Wk, bk, Wv, bv, ln_gamma, ln_beta):
        import jax, jax.numpy as jnp
        import numpy as np
        B, L, H = (8, 256, 128)
        SCALE = float(np.sqrt(H))
        EPS = 1e-05
        Q = queries @ Wq + bq
        K = keys @ Wk + bk
        V = values @ Wv + bv
        scores = jnp.einsum('bik,bjk->bij', Q, K) / SCALE
        scores = jnp.where(mask == 0, -jnp.inf, scores)
        probs = jax.nn.softmax(scores, axis=-1)
        context = jnp.einsum('bij,bjk->bik', probs, V)
        mu = jnp.mean(context, axis=-1, keepdims=True)
        var = jnp.var(context, axis=-1, keepdims=True)
        normed = (context - mu) * jax.lax.rsqrt(var + EPS)
        return normed * ln_gamma + ln_beta

    def _L2_ffn_ref(hidden_states, router_w, gate_w, up_w, down_w):
        import jax, jax.numpy as jnp
        import numpy as np
        S, B, H, I, E = (64, 2, 128, 352, 8)
        router_logits = jnp.einsum('sbh,eh->sbe', hidden_states, router_w)
        routing_indices = jnp.argmax(router_logits, axis=-1)
        out = jnp.zeros_like(hidden_states)
        for e in range(E):
            mask = (routing_indices == e)[..., None]
            xe = jnp.where(mask, hidden_states, 0.0)
            g = jnp.einsum('sbh,ih->sbi', xe, gate_w[e])
            u = jnp.einsum('sbh,ih->sbi', xe, up_w[e])
            ye = jnp.einsum('sbi,hi->sbh', jax.nn.silu(g) * u, down_w[e])
            out = out + jnp.where(mask, ye, 0.0)
        return out

    def _L3_xattn_ref(queries, keys, values, valid_lens, Wq, Wk, Wv, Wo):
        import jax, jax.numpy as jnp
        import numpy as np
        import math
        B, S, D, H = (2, 256, 128, 16)
        DH = D // H
        MASK_VALUE = -1000000.0

        def _split_heads(x):
            b, s, d = x.shape
            return x.reshape(b, s, H, DH).transpose(0, 2, 1, 3)
        q = _split_heads(queries @ Wq)
        k = _split_heads(keys @ Wk)
        v = _split_heads(values @ Wv)
        scores = jnp.einsum('bhqd,bhkd->bhqk', q, k) / math.sqrt(DH)
        mask = jnp.arange(scores.shape[-1])[None, None, None, :] < valid_lens[:, None, None, None]
        scores = jnp.where(mask, scores, MASK_VALUE)
        attn = jax.nn.softmax(scores, axis=-1)
        out = jnp.einsum('bhqk,bhkd->bhqd', attn, v)
        out = out.transpose(0, 2, 1, 3).reshape(queries.shape[0], queries.shape[1], D)
        return out @ Wo

    def _L3_ffn_ref(x, W_r, W_k, W_v, mu_r, mu_k):
        import jax, jax.numpy as jnp
        import numpy as np
        DIM = 128

        def _reference_tuple_inner(x, W_r, W_k, W_v, mu_r, mu_k):
            B, T, C = x.shape
            x_prev = jnp.concatenate([jnp.zeros((B, 1, C), x.dtype), x[:, :-1, :]], axis=1)
            xr = mu_r * x + (1.0 - mu_r) * x_prev
            xk = mu_k * x + (1.0 - mu_k) * x_prev
            r = jax.nn.sigmoid(jnp.einsum('btc,dc->btd', xr, W_r))
            k = jnp.einsum('btc,dc->btd', xk, W_k)
            k_act = jnp.square(jax.nn.relu(k))
            out = r * jnp.einsum('btc,dc->btd', k_act, W_v)
            new_state = x[:, -1, :]
            return (out, new_state)
        return _reference_tuple_inner(x, W_r, W_k, W_v, mu_r, mu_k)[0]
    x = x + jnp.tanh(g_xattn[0]) * _L0_xattn_ref(_layernorm(x, axis=-1), ctx_1024, ctx_1024, L0_xattn_Wq, L0_xattn_bq, L0_xattn_Wk, L0_xattn_bk, L0_xattn_Wv, L0_xattn_bv, L0_xattn_Wo, L0_xattn_bo)
    x = x + jnp.tanh(g_ffn[0]) * _L0_ffn_ref(_layernorm(x, axis=-1), L0_ffn_router_w, L0_ffn_rg, L0_ffn_ru, L0_ffn_rd, L0_ffn_sg, L0_ffn_su, L0_ffn_sd)
    x = x + jnp.tanh(g_xattn[1]) * _L1_xattn_ref(ctx_1024, ctx_1024, _layernorm(x, axis=-1), mask_Bx1xSxS2_ik1, L1_xattn_W_v, L1_xattn_W_o)
    x = x + jnp.tanh(g_ffn[1]) * _L1_ffn_ref(_layernorm(x, axis=-1), L1_ffn_gw, L1_ffn_gb, L1_ffn_w1, L1_ffn_b1, L1_ffn_w3, L1_ffn_b3, L1_ffn_w2, L1_ffn_b2, L1_ffn_sw1, L1_ffn_sb1, L1_ffn_sw3, L1_ffn_sb3, L1_ffn_sw2, L1_ffn_sb2)
    x = x + jnp.tanh(g_xattn[2]) * _L2_xattn_ref(_layernorm(x, axis=-1), ctx_1024, ctx_1024, mask_BxSxS2_ik1, L2_xattn_Wq, L2_xattn_bq, L2_xattn_Wk, L2_xattn_bk, L2_xattn_Wv, L2_xattn_bv, L2_xattn_ln_gamma, L2_xattn_ln_beta)
    x = x + jnp.tanh(g_ffn[2]) * _L2_ffn_ref(_layernorm(x, axis=-1), L2_ffn_router_w, L2_ffn_gate_w, L2_ffn_up_w, L2_ffn_down_w)
    x = x + jnp.tanh(g_xattn[3]) * _L3_xattn_ref(_layernorm(x, axis=-1), ctx_1024, ctx_1024, mask_B_ik0, L3_xattn_Wq, L3_xattn_Wk, L3_xattn_Wv, L3_xattn_Wo)
    x = x + jnp.tanh(g_ffn[3]) * _L3_ffn_ref(_layernorm(x, axis=-1), L3_ffn_W_r, L3_ffn_W_k, L3_ffn_W_v, L3_ffn_mu_r, L3_ffn_mu_k)
    return x

_drawn_inputs = setup_inputs


def setup_inputs(seed=0):
    import zlib

    import numpy as np

    out = dict(_drawn_inputs(seed))
    spreads = {'L0_xattn_bq': (0.0, 0.455),
     'L0_xattn_bk': (0.0, 2.0),
     'L0_xattn_bv': (0.0, 0.1),
     'L0_xattn_bo': (0.0, 0.1),
     'L1_ffn_gb': (0.0, 0.394),
     'L1_ffn_b1': (0.0, 0.733),
     'L1_ffn_b3': (0.0, 0.783),
     'L1_ffn_b2': (0.0, 0.455),
     'L1_ffn_sb1': (0.0, 0.1),
     'L1_ffn_sb3': (0.0, 0.1),
     'L1_ffn_sb2': (0.0, 0.1),
     'L2_xattn_bq': (0.0, 0.415),
     'L2_xattn_bk': (0.0, 2.0),
     'L2_xattn_bv': (0.0, 0.1),
     'L2_xattn_ln_gamma': (1.0, 0.2),
     'L2_xattn_ln_beta': (0.0, 0.1)}
    factors = {'g_ffn': 27.288,
     'L0_ffn_router_w': 8.0,
     'L0_ffn_rg': 8.0,
     'L0_ffn_ru': 8.0,
     'L0_ffn_rd': 8.0,
     'L0_ffn_sg': 4.688,
     'L0_ffn_su': 4.748,
     'L0_ffn_sd': 4.698,
     'L2_ffn_router_w': 8.0,
     'L2_ffn_gate_w': 8.0,
     'L2_ffn_up_w': 8.0,
     'L2_ffn_down_w': 8.0,
     'L3_ffn_W_r': 28.787,
     'L3_ffn_mu_r': 64.0,
     'L3_xattn_Wq': 2.676,
     'L3_xattn_Wk': 2.69,
     'L3_ffn_W_k': 4.634,
     'L3_ffn_W_v': 4.296,
     'L3_ffn_mu_k': 7.341}
    for name, (base, spread) in spreads.items():
        noise = np.random.default_rng([zlib.crc32(name.encode()), seed]).standard_normal(out[name].shape)
        drawn = base * np.exp(spread * noise) if base else spread * noise
        out[name] = jnp.asarray(drawn.astype(out[name].dtype))
    for name, factor in factors.items():
        out[name] = (out[name] * factor).astype(out[name].dtype)
    return out
```

```python
import numpy as np
from contextlib import ExitStack

import concourse.bass as bass
from concourse import mybir

F32 = mybir.dt.float32
F32R = mybir.dt.float32r
BF16 = mybir.dt.bfloat16
I32 = mybir.dt.int32
ALU = mybir.AluOpType
ACT = mybir.ActivationFunctionType
AX = mybir.AxisListType

B = 32
S = 100
D = 128
KEYS = 1444
HEADS = 16
DK = D // HEADS
GROUPS = 4
HALF = HEADS // 2
KT = -(-KEYS // D)
LAST = KEYS - (KT - 1) * D
UNITS = 2 * KT
CHUNKS = [(0, 482), (482, 482), (964, 480)]
NCH = len(CHUNKS)
BLK = 4
TOK = BLK * S
NBLK = B // BLK
FAR = -1.0e30


def bc(ap, axis, n):
    ap = ap.unsqueeze(axis)
    shape = list(ap.shape)
    shape[axis] = n
    return ap.broadcast_to(shape)


def needed(value):
    return not isinstance(value, int) or value > 0


def apart(eng, passed):
    eng.sem_inc(passed, 1)


class Memory:

    def __init__(self, nc, ctx, prefix):
        self.nc, self.ctx, self.prefix, self.sems = nc, ctx, prefix, []
        ctx.callback(self.clear)

    def sb(self, name, shape, dt=F32):
        return self.ctx.enter_context(self.nc.sbuf_tensor(f"{self.prefix}_{name}", shape, dt))

    def ps(self, name, shape, dt=F32):
        return self.ctx.enter_context(self.nc.psum_tensor(f"{self.prefix}_{name}", shape, dt))

    def sem(self, name):
        self.sems.append(self.nc.alloc_semaphore(f"{self.prefix}_{name}"))
        return self.sems[-1]

    def clear(self):
        with self.nc.Block() as block:

            @block.gpsimd
            def _(pool):
                self.nc.clear_and_free_semaphores(self.sems)


def batch(i, c):
    return (i, c)


def num(b):
    return b[0] * 2 + b[1] if not isinstance(b[0], int) else 2 * b[0] + b[1]


def par(b):
    return b[1] % 2


def nth(b):
    return b[0] + b[1] // 2


def nxt(b, n):
    return (b[0], b[1] + n)


def opening(b):
    return isinstance(b[0], int) and num(b) == 0


def rstd_steps(nc, dve, step, st, mean, rstd, tmp, var_ready, root_ready, eps):
    me, mo, m2e, m2o = st[:, :, 1], st[:, :, 4], st[:, :, 2], st[:, :, 5]
    ve, t, y = tmp[:, 0, :], tmp[:, 1, :], tmp[:, 2, :]
    step(nc.vector.tensor_tensor(t, me, mo, ALU.add))
    step(nc.vector.tensor_scalar(mean, t, 0.5, None, ALU.mult))
    step(nc.vector.tensor_tensor(t, me, mo, ALU.subtract))
    step(nc.vector.scalar_tensor_tensor(t, t, 0.25, t, ALU.mult, ALU.mult))
    step(nc.vector.tensor_tensor(ve, m2e, m2o, ALU.add))
    step(nc.vector.scalar_tensor_tensor(ve, ve, 1.0 / D, t, ALU.mult, ALU.add))
    nc.vector.tensor_scalar(ve, ve, eps, None, ALU.add).then_inc(var_ready, 1)
    dve.wait_ge(root_ready, 1)
    step(nc.vector.reciprocal(y, tmp[:, 3, :]))
    step(nc.vector.tensor_tensor(t, y, y, ALU.mult))
    step(nc.vector.tensor_tensor(t, t, ve, ALU.mult))
    step(nc.vector.tensor_scalar(t, t, -0.5, 1.5, ALU.mult, ALU.add))
    step(nc.vector.tensor_tensor(rstd, y, t, ALU.mult))


def layernorm_transposed(nc, name, x, xnT, ident):
    with ExitStack() as ctx:
        m = Memory(nc, ctx, name)
        st = m.sb("stats", [S, B, 6])
        mean = m.sb("mean", [S, B])
        rstd = m.sb("rstd", [S, B])
        tmp = m.sb("tmp", [S, 4, B])
        xn = m.sb("xn", [S, 2, BLK, D])
        pt = [m.ps(f"pt{i}", [D, TOK]) for i in range(2)]
        dve_step = m.sem("dve_step")
        var_ready = m.sem("var_ready")
        root_ready = m.sem("root_ready")
        xn_ready = m.sem("xn_ready")
        turned = m.sem("turned")
        stored = m.sem("stored")
        block = ctx.enter_context(nc.Block())

        @block.vector
        def _(dve):
            steps = [0]

            def step(ins):
                steps[0] += 1
                ins.then_inc(dve_step, 1)
                dve.wait_ge(dve_step, steps[0])

            with dve.Fori(0, NBLK) as n:
                for j in range(BLK):
                    nc.vector.bn_stats(st[:, n * BLK + j, :], x[:, n * BLK + j, :]).then_inc(dve_step, 1)
            steps[0] += B
            dve.wait_ge(dve_step, steps[0])
            rstd_steps(nc, dve, step, st, mean[:, :], rstd[:, :], tmp, var_ready, root_ready, 1e-5)
            with dve.Fori(0, NBLK // 2) as n:
                for p in range(2):
                    dve.wait_ge(turned, n * 2 * BLK + (p + 1) * BLK)
                    for j in range(BLK):
                        b = (n * 2 + p) * BLK + j
                        nc.vector.tensor_scalar(xn[:, p, j, :], x[:, b, :], mean[:, bass.ds(b, 1)],
                                                rstd[:, bass.ds(b, 1)], ALU.subtract, ALU.mult).then_inc(xn_ready, 1)

        @block.scalar
        def _(act):
            act.wait_ge(var_ready, 1)
            nc.scalar.activation(tmp[:, 3, :], tmp[:, 0, :], ACT.Sqrt).then_inc(root_ready, 1)
            with act.Fori(0, NBLK // 2) as n:
                for p in range(2):
                    act.wait_ge(turned, n * 2 * BLK + (p + 3) * BLK)
                    nc.scalar.activation(xnT[:, bass.ds((n * 2 + p) * TOK, TOK)], pt[p][:, :],
                                         ACT.Copy).then_inc(stored, 1)

        @block.tensor
        def _(pe):
            pe.sem_inc(turned, 2 * BLK)
            pe.sem_inc(stored, 2)
            with pe.Fori(0, NBLK // 2) as n:
                for p in range(2):
                    pe.wait_ge(stored, n * 2 + p + 1)
                    for j in range(BLK):
                        pe.wait_ge(xn_ready, (n * 2 + p) * BLK + j + 1)
                        nc.tensor.transpose(pt[p][:, j * S:(j + 1) * S], xn[:, p, j, :],
                                            ident[0:S, 0:S]).then_inc(turned, 1)


def attention_phase(nc, name, x, xnT, ident, w, dram, scale, gate, mask=None, lens=None):
    with ExitStack() as ctx:
        m = Memory(nc, ctx, name)
        sb, ps, sem = m.sb, m.ps, m.sem
        wq = sb("wq", [D, GROUPS, 96])
        wk = sb("wk", [D, D])
        wv = sb("wv", [D, D])
        wo = sb("wo", [D, D])
        blk = sb("blk", [D, 4 + HEADS])
        loads = [(wq[:, :, :], w["wq"]), (wk[:, :], w["wk"]), (wv[:, :], w["wv"]), (wo[:, :], w["wo"]),
                 (blk[:, :], w["blk"])]
        bq = bk = bv = bo = None
        if "bq" in w:
            bq = sb("bq", [96, GROUPS])
            bk = sb("bk", [D, 1])
            bv = sb("bv", [D, 1])
            bo = sb("bo", [1, D])
            loads += [(bq[:, :], w["bq"]), (bk[:, :], w["bk"]), (bv[:, :], w["bv"]), (bo[:, :], w["bo"])]
        ones_row = sb("ones_row", [1, S])
        ctxT = sb("ctxT", [D, 2, KT * D])
        kf = sb("kf", [D, KEYS])
        khi = sb("khi", [D, KEYS], F32R)
        klo = sb("klo", [D, KEYS], F32R)
        stack = sb("stack", [D, 2, GROUPS, KEYS], F32R)
        v_aug = sb("v_aug", [D, 2, KT, HEADS, 16])
        qf = sb("qf", [96, GROUPS, S])
        qs = sb("qs", [96, GROUPS, S], F32R)
        qblk = sb("qblk", [D, 2, HEADS, S], F32R)
        mx = sb("mx", [S, 2, HALF, NCH])
        nm = sb("nm", [S, 2, HALF])
        nmsp = sb("nmsp", [S, 2, 32], F32R)
        nsb = sb("nsb", [D, S])
        NP = 3
        probs = sb("probs", [D, NP, HALF * S])
        osb = sb("osb", [D, 2, 2 * S])
        rs = sb("rs", [S, 2, HALF])
        concat = sb("concat", [S, D])
        ctsb = sb("ctsb", [D, S])
        special = mask is not None or lens is not None
        if special:
            dump = sb("dump", [S, 2, 482])
        if mask is not None:
            mq_i = sb("mq_i", [S, KEYS], I32)
            mqf = sb("mqf", [S, 2, KEYS], BF16)
            mt_i = sb("mt_i", [D, KT * S], I32)
            gone = sb("gone", [D, 2, KT, S])
            pen = sb("pen", [D, 2, KT, S], BF16)
            identb = sb("identb", [D, D], BF16)
            usb = sb("usb", [S, 2, HEADS, 9])
            nneg = sb("nneg", [S, 2, HALF])
            em = sb("em", [S, 2, HEADS])
            acc = sb("acc", [S, 2, HALF, 9])
            t1 = sb("t1", [S, 2, HALF, 9])
        if lens is not None:
            iota_q = sb("iota_q", [S, KEYS])
            penq = sb("penq", [S, 2, KEYS])
            vl_i = sb("vl_i", [D, B], I32)
            vl = sb("vl", [D, B])
            alive = sb("alive", [D, B])
            keyno = sb("keyno", [D, KT])
            kbias = sb("kbias", [D, B, KT])
            loads += [(vl_i[:, :], lens.partition_broadcast(D)), (keyno[:, :], w["keyno"]),
                      (iota_q[:, :], w["iota"].partition_broadcast(S))]
        p_sc = [ps(f"scores{i}", [D, 2, 512]) for i in range(2)]
        p_pv = ps("pv", [D, 512])
        p_mx = [ps(f"max{i}", [S, 512]) for i in range(2)]
        p_rest = ps("rest", [D, 512])

        passed = {e: sem("passed_" + e) for e in ("sp", "pool", "act", "dve", "pe")}
        weights_in = sem("weights_in")
        consts_ready = sem("consts_ready")
        ctx_in = [sem(f"ctx_in{i}") for i in range(2)]
        stack_in = [[sem(f"stack_in{i}{h}") for h in range(2)] for i in range(2)]
        k_chunk = sem("k_chunk")
        k_rounded = sem("k_rounded")
        klo_ready = sem("klo_ready")
        v_chunk = sem("v_chunk")
        v_ready = sem("v_ready")
        q_chunk = sem("q_chunk")
        qf_ready = sem("qf_ready")
        qs_ready = sem("qs_ready")
        ql_ready = sem("ql_ready")
        qblk_ready = sem("qblk_ready")
        max_scores = sem("max_scores")
        maxed = sem("maxed")
        negm_ready = sem("negm_ready")
        neg_turned = sem("neg_turned")
        nsb_ready = sem("nsb_ready")
        qneg_ready = sem("qneg_ready")
        scores_ready = sem("scores_ready")
        probs_ready = sem("probs_ready")
        pv_done = sem("pv_done")
        pv_out = sem("pv_out")
        out_turned = sem("out_turned")
        norm_ready = sem("norm_ready")
        concat_turned = sem("concat_turned")
        concat_ready = sem("concat_ready")
        wo_ready = sem("wo_ready")
        x_done = sem("x_done")
        dve_step = sem("dve_step")
        if mask is not None:
            maskq_in, maskt_in = sem("maskq_in"), sem("maskt_in")
            maskq_ready, gone_ready, pen_ready = sem("maskq_ready"), sem("gone_ready"), sem("pen_ready")
            u_chunk, usb_ready, nneg_ready, em_ready = sem("u_chunk"), sem("usb_ready"), sem("nneg_ready"), sem("em_ready")
        if lens is not None:
            penq_ready = sem("penq_ready")

        block = ctx.enter_context(nc.Block())
        LOADED = 16 * len(loads)
        V_AT, U_AT, K_AT, Q_AT = ((7, 8, 9), 10, (14, 15, 16), 17) if mask is None else ((7, 9, 11), 12, (14, 16, 18), 19)
        CONSTS = 5 + (1 if lens is not None else 0)

        def stack_load(eng, b, h):
            eng.wait_ge(klo_ready, num(b) + 1)
            apart(eng, passed["sp"])
            if needed(UNITS * (num(b) - 2) + KT * (h + 1)):
                eng.wait_ge(scores_ready, UNITS * (num(b) - 2) + KT * (h + 1))
            for g in (2 * h, 2 * h + 1):
                for part, src in enumerate((khi, klo, khi)):
                    eng.dma_start(stack[32 * part:32 * part + 32, par(b), g, :].bitcast(F32),
                                  src[32 * g:32 * g + 32, :].bitcast(F32)).then_inc(stack_in[par(b)][h], 16)

        def stack_there(eng, b, h):
            eng.wait_ge(stack_in[par(b)][h], (nth(b) + 1) * 96)

        def ctx_load(eng, b):
            if needed((num(b) - 2) * 3 + 3):
                eng.wait_ge(v_chunk, (num(b) - 2) * 3 + 3)
            eng.dma_start(ctxT[:, par(b), 0:KEYS], dram["ctxT"][num(b)]).then_inc(ctx_in[par(b)], 16)

        def mask_loads(eng, b, rows, cols):
            if mask is None:
                return
            if rows:
                if needed(num(b)):
                    eng.wait_ge(maskq_ready, num(b))
                eng.dma_start(mq_i[:, :], mask[0][num(b)]).then_inc(maskq_in, 16)
            if cols:
                if needed(num(b)):
                    eng.wait_ge(gone_ready, num(b))
                eng.dma_start(mt_i[:, :], mask[1][num(b)]).then_inc(maskt_in, 16)

        @block.sync
        def _(sp):
            for dst, src in loads:
                sp.dma_start(dst, src).then_inc(weights_in, 16)
            ctx_load(sp, batch(0, 0))
            ctx_load(sp, batch(0, 1))
            mask_loads(sp, batch(0, 0), True, True)
            stack_load(sp, batch(0, 0), 0)
            stack_load(sp, batch(0, 0), 1)
            mask_loads(sp, batch(0, 1), True, True)
            stack_load(sp, batch(0, 1), 0)
            ctx_load(sp, batch(0, 2))
            mask_loads(sp, batch(0, 2), True, False)

            def iteration(b, ahead):
                if ahead >= 1:
                    stack_load(sp, nxt(b, 1), 1)
                if ahead >= 2:
                    mask_loads(sp, nxt(b, 2), False, True)
                if ahead >= 3:
                    ctx_load(sp, nxt(b, 3))
                if ahead >= 2:
                    stack_load(sp, nxt(b, 2), 0)
                if ahead >= 3:
                    mask_loads(sp, nxt(b, 3), True, False)

            iteration(batch(0, 0), 3)
            iteration(batch(0, 1), 3)
            iteration(batch(0, 2), 3)
            with sp.Fori(0, (B - 6) // 2) as i:
                iteration(batch(i, 3), 3)
                iteration(batch(i, 4), 3)
            for c in range(B - 3, B):
                iteration(batch(0, c), B - 1 - c)

        @block.gpsimd
        def _(pool):
            pool.memset(ctxT[:, :, KEYS:KT * D], 0.0).then_inc(consts_ready, 1)
            pool.memset(v_aug[:, :, :, :, 8:16], 0.0).then_inc(ql_ready, 1)
            pool.wait_ge(ql_ready, 1)
            pool.memset(v_aug[:, :, :, :, 8:9], 1.0).then_inc(consts_ready, 1)

            def k_low(b):
                if needed(2 * num(b) - 1):
                    pool.wait_ge(qneg_ready, 2 * num(b) - 1)
                pool.wait_ge(k_rounded, num(b) * NCH + NCH)
                pool.tensor_tensor(klo[:, :], kf[:, :], khi[:, :].bitcast(F32), ALU.subtract).then_inc(klo_ready, 1)

            def q_low(b):
                pool.wait_ge(qs_ready, num(b) + 1)
                pool.wait_ge(klo_ready, num(b) + 1)
                pool.tensor_tensor(qs[64:96, :, :], qf[64:96, :, :], qs[64:96, :, :].bitcast(F32),
                                   ALU.subtract).then_inc(ql_ready, 1)

            def q_spread(b, h):
                pool.wait_ge(ql_ready, num(b) + 2)
                if h == 1:
                    if needed(2 * num(b)):
                        pool.wait_ge(qneg_ready, 2 * num(b))
                if needed(UNITS * (num(b) - 2) + KT * (h + 1)):
                    pool.wait_ge(scores_ready, UNITS * (num(b) - 2) + KT * (h + 1))
                for g in range(2):
                    ins = pool.tensor_tensor(
                        qblk[0:96, par(b), HALF * h + 4 * g:HALF * h + 4 * g + 4, :],
                        bc(qs[:, 2 * h + g, :].bitcast(F32), 1, 4), bc(blk[0:96, 0:4], 2, S), ALU.mult)
                ins.then_inc(qblk_ready, 1)

            def neg_spread(b, h, last=False):
                pool.wait_ge(nsb_ready, 2 * num(b) + h + 1)
                pool.wait_ge(qblk_ready, 2 * num(b) + (3 if h == 1 and not last else 2))
                if mask is not None:
                    pool.wait_ge(gone_ready, num(b) + 1)
                pool.tensor_tensor(qblk[96:128, par(b), HALF * h:HALF * h + HALF, :],
                                   bc(nsb[96:128, :], 1, HALF), bc(blk[96:128, 4 + HALF * h:4 + HALF * h + HALF], 2, S),
                                   ALU.mult).then_inc(qneg_ready, 1)

            def gone_keys(b):
                if mask is None:
                    return
                pool.wait_ge(maskt_in, num(b) * 16 + 16)
                if needed(UNITS * (num(b) - 2) + UNITS):
                    pool.wait_ge(pv_done, UNITS * (num(b) - 2) + UNITS)
                if needed(num(b) - 1):
                    pool.wait_ge(pen_ready, num(b) - 1)
                pool.wait_ge(qblk_ready, 2 * num(b) + 2)
                apart(pool, passed["pool"])
                pool.tensor_scalar(gone[:, par(b), :, :], mt_i[:, :].rearrange("p (t q) -> p t q", t=KT), 0.0, None,
                                   ALU.is_equal).then_inc(gone_ready, 1)

            pool.wait_ge(weights_in, LOADED)
            k_low(batch(0, 0))
            q_low(batch(0, 0))
            q_spread(batch(0, 0), 0)
            q_spread(batch(0, 0), 1)
            gone_keys(batch(0, 0))
            neg_spread(batch(0, 0), 0)
            k_low(batch(0, 1))
            q_low(batch(0, 1))
            q_spread(batch(0, 1), 0)

            def iteration(b, ahead):
                neg_spread(b, 1, ahead == 0)
                if ahead >= 1:
                    q_spread(nxt(b, 1), 1)
                    gone_keys(nxt(b, 1))
                    neg_spread(nxt(b, 1), 0)
                if ahead >= 2:
                    k_low(nxt(b, 2))
                    q_low(nxt(b, 2))
                    q_spread(nxt(b, 2), 0)

            iteration(batch(0, 0), 2)
            iteration(batch(0, 1), 2)
            iteration(batch(0, 2), 2)
            with pool.Fori(0, (B - 6) // 2) as i:
                iteration(batch(i, 3), 2)
                iteration(batch(i, 4), 2)
            for c in range(B - 3, B):
                iteration(batch(0, c), B - 1 - c)

        @block.scalar
        def _(act):
            act.wait_ge(weights_in, LOADED)
            act.wait_ge(consts_ready, CONSTS)

            def k_evac(b, c):
                o, n = CHUNKS[c]
                act.wait_ge(k_chunk, num(b) * NCH + c + 1)
                if c == 0:
                    if needed(num(b)):
                        act.wait_ge(klo_ready, num(b))
                    for h in range(2):
                        if not (isinstance(b[0], int) and b[0] == 0 and b[1] == 0):
                            stack_there(act, nxt(b, -1), h)
                if bk is not None:
                    act.activation(kf[:, o:o + n], p_rest[:, 0:n], ACT.Identity, bias=bk[:, 0:1])
                    act.activation(khi[:, o:o + n], p_rest[:, 0:n], ACT.Identity,
                                   bias=bk[:, 0:1]).then_inc(k_rounded, 1)
                else:
                    act.activation(kf[:, o:o + n], p_rest[:, 0:n], ACT.Copy)
                    act.activation(khi[:, o:o + n], p_rest[:, 0:n], ACT.Copy).then_inc(k_rounded, 1)

            def q_round(b):
                act.wait_ge(qf_ready, num(b) + 1)
                if needed(2 * num(b)):
                    act.wait_ge(qblk_ready, 2 * num(b))
                act.activation(qs[:, :, :], qf[:, :, :], ACT.Copy).then_inc(qs_ready, 1)

            def v_evac(b, c):
                act.wait_ge(v_chunk, num(b) * 3 + c + 1)
                if c == 0:
                    if needed(UNITS * (num(b) - 2) + UNITS):
                        act.wait_ge(pv_done, UNITS * (num(b) - 2) + UNITS)
                act.activation(v_aug[:, par(b), 4 * c:4 * c + 4, :, 0:DK],
                               p_rest[:, :].rearrange("p (t h d) -> p t h d", t=4, h=HEADS),
                               ACT.Copy).then_inc(v_ready, 1)

            def neg_evac(b, h):
                act.wait_ge(neg_turned, 2 * num(b) + h + 1)
                if needed(2 * num(b) + h):
                    act.wait_ge(qneg_ready, 2 * num(b) + h)
                act.activation(nsb[96:128, :], p_rest[96:128, 0:S], ACT.Copy).then_inc(nsb_ready, 1)

            def pv_evac(b, h):
                act.wait_ge(pv_done, UNITS * num(b) + KT * (h + 1))
                if needed(num(b)):
                    act.wait_ge(out_turned, num(b))
                act.activation(osb[:, h, :], p_pv[:, 0:2 * S], ACT.Copy).then_inc(pv_out, 1)

            def concat_evac(b):
                act.wait_ge(concat_turned, num(b) + 1)
                if needed(num(b)):
                    act.wait_ge(wo_ready, num(b))
                if bv is not None:
                    act.activation(ctsb[:, :], p_rest[:, 0:S], ACT.Identity, bias=bv[:, 0:1]).then_inc(concat_ready, 1)
                else:
                    act.activation(ctsb[:, :], p_rest[:, 0:S], ACT.Copy).then_inc(concat_ready, 1)

            def exps(b, u):
                h, kt = divmod(u, KT)
                rows = D if kt < KT - 1 else LAST
                act.wait_ge(scores_ready, UNITS * num(b) + u + 1)
                if needed(UNITS * num(b) + u - NP + 1):
                    act.wait_ge(pv_done, UNITS * num(b) + u - NP + 1)
                out_ = probs[0:rows, u % NP, :].rearrange("p (g n) -> p g n", g=2)
                in_ = p_sc[u % 2][0:rows, :, 0:4 * S]
                if lens is not None:
                    apart(act, passed["act"])
                    act.activation(out_, in_, ACT.Exp, bias=kbias[0:rows, bass.ds(num(b), 1), kt], scale=scale)\
                       .then_inc(probs_ready, 1)
                else:
                    act.activation(out_, in_, ACT.Exp, scale=scale).then_inc(probs_ready, 1)

            def pen_make(b):
                if mask is None:
                    return
                act.wait_ge(gone_ready, num(b) + 1)
                act.activation(pen[:, par(b), :, :], gone[:, par(b), :, :], ACT.Copy, scale=FAR).then_inc(pen_ready, 1)

            def u_evac(b):
                if mask is None:
                    return
                act.wait_ge(u_chunk, num(b) + 1)
                if needed(num(b) - 1):
                    act.wait_ge(norm_ready, num(b) - 1)
                act.activation(usb[:, par(b), :, :].rearrange("p h d -> p (h d)"), p_rest[0:S, 0:HEADS * 9],
                               ACT.Copy).then_inc(usb_ready, 1)

            def em_make(b, h):
                if mask is None:
                    return
                act.wait_ge(nneg_ready, 2 * num(b) + h + 1)
                if needed(num(b) - 1):
                    act.wait_ge(norm_ready, num(b) - 1)
                act.activation(em[:, par(b), HALF * h:HALF * h + HALF], nneg[:, h, :], ACT.Exp,
                               scale=scale).then_inc(em_ready, 1)

            b0, b1 = batch(0, 0), batch(0, 1)
            for c in range(NCH):
                k_evac(b0, c)
            q_round(b0)
            pen_make(b0)
            neg_evac(b0, 0)
            em_make(b0, 0)
            em_make(b0, 1)
            for c in range(NCH):
                k_evac(b1, c)
            q_round(b1)
            for c in range(3):
                v_evac(b0, c)
            u_evac(b0)

            def iteration(b, first, ahead):
                for u in range(UNITS):
                    if u == 1:
                        if not first:
                            pv_evac(nxt(b, -1), 1)
                        neg_evac(b, 1)
                    if u == 4 and not first:
                        concat_evac(nxt(b, -1))
                    if ahead >= 1 and u in V_AT:
                        v_evac(nxt(b, 1), V_AT.index(u))
                    if ahead >= 1 and u == U_AT:
                        pen_make(nxt(b, 1))
                        u_evac(nxt(b, 1))
                    if u == 13:
                        pv_evac(b, 0)
                        if ahead >= 1:
                            neg_evac(nxt(b, 1), 0)
                            em_make(nxt(b, 1), 0)
                    if ahead >= 2 and u in K_AT:
                        k_evac(nxt(b, 2), K_AT.index(u))
                    if ahead >= 2 and u == Q_AT + 1:
                        q_round(nxt(b, 2))
                    exps(b, u)
                if ahead >= 1:
                    em_make(nxt(b, 1), 1)

            iteration(b0, True, 2)
            iteration(batch(0, 1), False, 2)
            iteration(batch(0, 2), False, 2)
            with act.Fori(0, (B - 6) // 2) as i:
                iteration(batch(i, 3), False, 2)
                iteration(batch(i, 4), False, 2)
            for c in range(B - 3, B):
                iteration(batch(0, c), False, B - 1 - c)
            last = batch(0, B - 1)
            pv_evac(last, 1)
            concat_evac(last)

        @block.vector
        def _(dve):
            steps = {"at": 0, "loop": 0}

            def step(ins):
                steps["at"] += 1
                ins.then_inc(dve_step, 1)
                dve.wait_ge(dve_step, steps["loop"] + steps["at"])

            nc.vector.memset(stack[96:128, 0, :, :].bitcast(F32), 1.0).then_inc(consts_ready, 1)
            nc.vector.memset(nmsp[:, :, :].bitcast(F32), 0.0).then_inc(consts_ready, 1)
            nc.vector.memset(ones_row[:, :], 1.0).then_inc(consts_ready, 1)
            dve.wait_ge(weights_in, LOADED)
            if mask is not None:
                step(nc.vector.tensor_copy(identb[:, :], ident[:, :]))
            if lens is not None:
                step(nc.vector.tensor_copy(vl[:, :], vl_i[:, :]))
                step(nc.vector.tensor_scalar(alive[:, :], vl[:, :], 0.0, None, ALU.is_gt))
                step(nc.vector.tensor_tensor(xnT[:, :].rearrange("p (b s) -> p b s", b=B),
                                             xnT[:, :].rearrange("p (b s) -> p b s", b=B),
                                             bc(alive[:, :], 2, S), ALU.mult))
                step(nc.vector.tensor_tensor(kbias[:, :, :], bc(keyno[:, :], 1, B), bc(vl[:, :], 2, KT), ALU.is_ge))
                nc.vector.tensor_scalar(kbias[:, :, :], kbias[:, :, :], -1.0e6, None, ALU.mult).then_inc(consts_ready, 1)
            dve.wait_ge(consts_ready, CONSTS)

            def q_bias(b):
                dve.wait_ge(q_chunk, num(b) + 1)
                if needed(2 * num(b)):
                    dve.wait_ge(qblk_ready, 2 * num(b))
                src = p_rest[0:96, 0:GROUPS * S].rearrange("p (g s) -> p g s", g=GROUPS)
                if bq is not None:
                    nc.vector.tensor_tensor(qf[:, :, :], src, bc(bq[:, :], 2, S), ALU.add).then_inc(qf_ready, 1)
                else:
                    nc.vector.tensor_copy(qf[:, :, :], src).then_inc(qf_ready, 1)

            def mask_rows(b):
                if mask is not None:
                    dve.wait_ge(maskq_in, num(b) * 16 + 16)
                    if needed((num(b) - 1) * 2 * HALF * NCH):
                        dve.wait_ge(maxed, (num(b) - 1) * 2 * HALF * NCH)
                    nc.vector.tensor_scalar(mqf[:, par(b), :], mq_i[:, :], 0.0, None,
                                            ALU.not_equal).then_inc(maskq_ready, 1)
                if lens is not None:
                    if needed((num(b) - 1) * 2 * HALF * NCH):
                        dve.wait_ge(maxed, (num(b) - 1) * 2 * HALF * NCH)
                    nc.vector.tensor_scalar(penq[:, par(b), :], iota_q[:, :], vl[0:S, bass.ds(num(b), 1)],
                                            -1.0e6 / scale, ALU.is_ge, ALU.mult).then_inc(penq_ready, 1)

            def reduce_max(b, h, k):
                head, c = divmod(k, NCH)
                o, n = CHUNKS[c]
                at = 2 * HALF * NCH * num(b) + HALF * NCH * h + k
                dve.wait_ge(max_scores, at + 1)
                src, out_ = p_mx[k % 2][:, 0:n], mx[:, h, head, c:c + 1]
                if not special:
                    nc.vector.tensor_reduce(out_, src, AX.X, ALU.max).then_inc(maxed, 1)
                    return
                if needed(at - 1):
                    dve.wait_ge(maxed, at - 1)
                if mask is not None:
                    if h == 0 and k == 0:
                        dve.wait_ge(maskq_ready, num(b) + 1)
                    apart(dve, passed["dve"])
                    nc.vector.tensor_tensor_reduce(dump[:, k % 2, 0:n], src, mqf[:, par(b), o:o + n], 1.0, -3.0e38,
                                                   ALU.mult, ALU.max, out_).then_inc(maxed, 1)
                else:
                    if h == 0 and k == 0:
                        dve.wait_ge(penq_ready, num(b) + 1)
                    apart(dve, passed["dve"])
                    nc.vector.tensor_tensor_reduce(dump[:, k % 2, 0:n], src, penq[:, par(b), o:o + n], 1.0, -3.0e38,
                                                   ALU.add, ALU.max, out_).then_inc(maxed, 1)

            def negate_max(b, h):
                dve.wait_ge(maxed, 2 * HALF * NCH * num(b) + HALF * NCH * (h + 1))
                if needed(2 * num(b) - 1 + h):
                    dve.wait_ge(neg_turned, 2 * num(b) - 1 + h)
                step(nc.vector.tensor_reduce(nm[:, h, :], mx[:, h, :, :], AX.X, ALU.max, negate=True))
                hi = nmsp[:, h, HALF * h:HALF * h + HALF]
                step(nc.vector.tensor_copy(hi, nm[:, h, :]))
                nc.vector.tensor_tensor(nmsp[:, h, HEADS + HALF * h:HEADS + HALF * h + HALF], nm[:, h, :],
                                        hi.bitcast(F32), ALU.subtract).then_inc(negm_ready, 1)
                if mask is not None:
                    if needed(2 * num(b) - 1 + h):
                        dve.wait_ge(em_ready, 2 * num(b) - 1 + h)
                    nc.vector.tensor_scalar(nneg[:, h, :], nm[:, h, :], 0.0, None, ALU.min).then_inc(nneg_ready, 1)

            turned = p_rest[0:S, :].rearrange("p (a t c) -> p a t c", a=2, c=32)

            def normalise(b):
                dve.wait_ge(out_turned, num(b) + 1)
                if needed(num(b)):
                    dve.wait_ge(concat_turned, num(b))
                cc = concat[:, :].rearrange("p (t a d) -> p a t d", a=2, d=DK)
                for a in range(2):
                    src = turned[:, a, :, 16 * a:16 * a + 9]
                    if mask is not None:
                        if a == 0:
                            dve.wait_ge(usb_ready, num(b) + 1)
                            dve.wait_ge(em_ready, 2 * num(b) + 2)
                        emv = em[:, par(b), :].rearrange("p (t a) -> p a t", a=2)[:, a, :]
                        uv = usb[:, par(b), :, :].rearrange("p (t a) d -> p a t d", a=2)[:, a, :, :]
                        step(nc.vector.tensor_tensor(t1[:, a, :, :], uv, bc(emv, 2, 9), ALU.mult))
                        step(nc.vector.tensor_tensor(acc[:, a, :, :], src, t1[:, a, :, :], ALU.add))
                        src = acc[:, a, :, :]
                    step(nc.vector.reciprocal(rs[:, a, :], src[:, :, 8]))
                    ins = nc.vector.tensor_tensor(cc[:, a, :, :], src[:, :, 0:DK], bc(rs[:, a, :], 2, DK), ALU.mult)
                ins.then_inc(norm_ready, 1)

            def update_x(b):
                dve.wait_ge(wo_ready, num(b) + 1)
                at = x[:, :, :].rearrange("p b d -> p (b d)")[:, bass.ds(num(b) * D, D)]
                nc.vector.scalar_tensor_tensor(at, p_rest[0:S, 0:D], gate, at, ALU.mult, ALU.add).then_inc(x_done, 1)

            b0, b1 = batch(0, 0), batch(0, 1)
            q_bias(b0)
            mask_rows(b0)
            for h in range(2):
                for k in range(HALF * NCH):
                    reduce_max(b0, h, k)
                negate_max(b0, h)
            nc.vector.memset(stack[96:128, 1, :, :].bitcast(F32), 1.0).then_inc(consts_ready, 1)
            q_bias(b1)
            mask_rows(b1)

            def iteration(b, first, ahead):
                for u in range(UNITS):
                    h, kt = divmod(u, KT)
                    if u == 2 and not first:
                        normalise(nxt(b, -1))
                    if u == 6 and not first:
                        update_x(nxt(b, -1))
                    if ahead >= 2 and u == Q_AT:
                        q_bias(nxt(b, 2))
                    if ahead >= 2 and u == Q_AT + 2:
                        mask_rows(nxt(b, 2))
                    if ahead >= 1:
                        reduce_max(nxt(b, 1), h, 2 * kt)
                        reduce_max(nxt(b, 1), h, 2 * kt + 1)
                        if kt == KT - 1:
                            negate_max(nxt(b, 1), h)

            iteration(b0, True, 2)
            iteration(batch(0, 1), False, 2)
            iteration(batch(0, 2), False, 2)
            per = 4 + (6 if mask is not None else 2)
            with dve.Fori(0, (B - 6) // 2) as i:
                start = steps["at"]
                steps["loop"] = i * (2 * per)
                iteration(batch(i, 3), False, 2)
                iteration(batch(i, 4), False, 2)
                assert steps["at"] == start + 2 * per
            steps["loop"] = ((B - 6) // 2 - 1) * 2 * per
            for c in range(B - 3, B):
                iteration(batch(0, c), False, B - 1 - c)
            last = batch(0, B - 1)
            normalise(last)
            update_x(last)

        @block.tensor
        def _(pe):
            pe.wait_ge(weights_in, LOADED)

            def k_proj(b, c, before):
                o, n = CHUNKS[c]
                if needed(before[1]):
                    pe.wait_ge(*before)
                if c == 0:
                    pe.wait_ge(ctx_in[par(b)], (nth(b) + 1) * 16)
                pe.matmul(p_rest[:, 0:n], wk[:, :], ctxT[:, par(b), o:o + n], start=True, stop=True).then_inc(k_chunk, 1)

            def k_taken(b, c=NCH - 1):
                return k_rounded, num(b) * NCH + c + 1

            def q_proj(b, before):
                pe.wait_ge(*before)
                for g in range(GROUPS):
                    ins = pe.matmul(p_rest[0:96, g * S:(g + 1) * S], wq[:, g, :], xnT[:, bass.ds(num(b) * S, S)],
                                    start=True, stop=True)
                ins.then_inc(q_chunk, 1)

            def v_proj(b, c, before):
                pe.wait_ge(*before)
                for t in range(4):
                    o = (4 * c + t) * D
                    ins = pe.matmul(p_rest[:, t * D:(t + 1) * D], ctxT[:, par(b), o:o + D], wv[:, :],
                                    start=True, stop=True)
                ins.then_inc(v_chunk, 1)

            def u_proj(b, before):
                if mask is None:
                    return
                pe.wait_ge(*before)
                pe.wait_ge(gone_ready, num(b) + 1)
                for t in range(KT):
                    r = D if t < KT - 1 else LAST
                    ins = pe.matmul(p_rest[0:S, 0:HEADS * 9].rearrange("p (h d) -> p h d", h=HEADS),
                                    gone[0:r, par(b), t, :], v_aug[0:r, par(b), t, :, 0:9],
                                    start=(t == 0), stop=(t == KT - 1))
                ins.then_inc(u_chunk, 1)

            def neg_turn(b, h, before):
                pe.wait_ge(*before)
                pe.wait_ge(negm_ready, 2 * num(b) + h + 1)
                pe.matmul(p_rest[96:128, 0:S], nmsp[:, h, :].bitcast(F32), ident[0:S, 0:S],
                          start=True, stop=True).then_inc(neg_turned, 1)

            def max_mm(b, h, k):
                head, c = divmod(k, NCH)
                o, n = CHUNKS[c]
                at = 2 * HALF * NCH * num(b) + HALF * NCH * h + k
                if k == 0:
                    stack_there(pe, b, h)
                    pe.wait_ge(qblk_ready, 2 * num(b) + h + 1)
                if needed(at - 1):
                    pe.wait_ge(maxed, at - 1)
                g = 2 * h + head // 4
                pe.matmul(p_mx[k % 2][:, 0:n], qblk[0:96, par(b), HALF * h + head, :], stack[0:96, par(b), g, o:o + n],
                          start=True, stop=True).then_inc(max_scores, 1)

            def score_mm(b, u):
                h, kt = divmod(u, KT)
                r = D if kt < KT - 1 else LAST
                if kt == 0:
                    pe.wait_ge(qneg_ready, 2 * num(b) + h + 1)
                if u == 0 and mask is not None:
                    pe.wait_ge(pen_ready, num(b) + 1)
                if needed(UNITS * num(b) + u - 1):
                    pe.wait_ge(probs_ready, UNITS * num(b) + u - 1)
                for g in range(2):
                    out_ = p_sc[u % 2][0:r, g, 0:4 * S]
                    ins = pe.matmul(out_, stack[:, par(b), 2 * h + g, kt * D:kt * D + r],
                                    qblk[:, par(b), HALF * h + 4 * g:HALF * h + 4 * g + 4, :].rearrange("p h s -> p (h s)"),
                                    start=True, stop=mask is None)
                    if mask is not None:
                        ins = pe.matmul(out_.rearrange("p (h s) -> p h s", h=4), identb[0:r, 0:r],
                                        bc(pen[0:r, par(b), kt, :], 1, 4), start=False, stop=True)
                ins.then_inc(scores_ready, 1)

            def pv_mm(b, u):
                h, kt = divmod(u, KT)
                r = D if kt < KT - 1 else LAST
                pe.wait_ge(probs_ready, UNITS * num(b) + u + 1)
                if kt == 0:
                    if needed(2 * num(b) + h):
                        pe.wait_ge(pv_out, 2 * num(b) + h)
                if u == 0:
                    pe.wait_ge(v_ready, 3 * num(b) + 3)
                if kt == KT - 1:
                    apart(pe, passed["pe"])
                for t in range(4):
                    head = HALF * h + 2 * t
                    ins = pe.matmul(p_pv[32 * t:32 * t + 32, 0:2 * S],
                                    v_aug[0:r, par(b), kt, head:head + 2, :].rearrange("p h d -> p (h d)"),
                                    probs[0:r, u % NP, 2 * t * S:2 * (t + 1) * S],
                                    start=(kt == 0), stop=(kt == KT - 1))
                ins.then_inc(pv_done, 1)

            def out_turn(b, before):
                pe.wait_ge(*before)
                pe.wait_ge(pv_out, 2 * num(b) + 2)
                for a in range(2):
                    for h in range(2):
                        ins = pe.transpose(p_rest[0:S, a * 256 + h * D:a * 256 + (h + 1) * D],
                                           osb[:, h, a * S:(a + 1) * S], ident[:, :])
                ins.then_inc(out_turned, 1)

            def concat_turn(b):
                pe.wait_ge(norm_ready, num(b) + 1)
                pe.transpose(p_rest[:, 0:S], concat[:, :], ident[0:S, 0:S]).then_inc(concat_turned, 1)

            def out_proj(b):
                pe.wait_ge(concat_ready, num(b) + 1)
                ins = pe.matmul(p_rest[0:S, 0:D], ctsb[:, :], wo[:, :], start=True, stop=bo is None)
                if bo is not None:
                    ins = pe.matmul(p_rest[0:S, 0:D], ones_row[:, :], bo[:, :], start=False, stop=True)
                ins.then_inc(wo_ready, 1)

            b0, b1 = batch(0, 0), batch(0, 1)
            for c in range(NCH):
                k_proj(b0, c, k_taken(b0, c - 1))
            q_proj(b0, k_taken(b0))
            pe.wait_ge(consts_ready, CONSTS)
            for h in range(2):
                for k in range(HALF * NCH):
                    max_mm(b0, h, k)
            neg_turn(b0, 0, (qf_ready, 1))
            for c in range(NCH):
                k_proj(b1, c, (nsb_ready, 1) if c == 0 else k_taken(b1, c - 1))
            q_proj(b1, k_taken(b1))
            for c in range(3):
                v_proj(b0, c, (qf_ready, 2) if c == 0 else (v_ready, c))
            u_proj(b0, (v_ready, 3))

            def iteration(b, first, ahead):
                b1, b2 = nxt(b, 1), nxt(b, 2)
                v_taken = (usb_ready, num(b1) + 1) if mask is not None else (v_ready, 3 * num(b1) + 3)
                for u in range(UNITS):
                    h, kt = divmod(u, KT)
                    if u == 1:
                        if first:
                            before = (usb_ready, 1) if mask is not None else (v_ready, 3)
                        elif ahead >= 1:
                            before = (qf_ready, num(b1) + 1)
                        else:
                            before = (nsb_ready, 2 * num(b) + 1)
                        neg_turn(b, 1, before)
                    if u == 2 and not first:
                        out_turn(nxt(b, -1), (nsb_ready, 2 * num(b) + 2))
                    if u == 4 and not first:
                        concat_turn(nxt(b, -1))
                    if u == 6 and not first:
                        out_proj(nxt(b, -1))
                    if ahead >= 1 and u in V_AT:
                        c = V_AT.index(u)
                        before = (v_ready, 3 * num(b1) + c)
                        if c == 0:
                            before = (nsb_ready, 2) if first else (x_done, num(b))
                        v_proj(b1, c, before)
                    if ahead >= 1 and u == U_AT:
                        u_proj(b1, (v_ready, 3 * num(b1) + 3))
                    if ahead >= 1 and u == 13:
                        neg_turn(b1, 0, v_taken)
                    if ahead >= 2 and u in K_AT:
                        c = K_AT.index(u)
                        k_proj(b2, c, (nsb_ready, 2 * num(b1) + 1) if c == 0 else k_taken(b2, c - 1))
                    if ahead >= 2 and u == Q_AT:
                        q_proj(b2, k_taken(b2))
                    score_mm(b, u)
                    if ahead >= 1:
                        max_mm(b1, h, 2 * kt)
                    if u > 0:
                        pv_mm(b, u - 1)
                    elif not first:
                        pv_mm(nxt(b, -1), UNITS - 1)
                    if ahead >= 1:
                        max_mm(b1, h, 2 * kt + 1)

            iteration(b0, True, 2)
            pe.wait_ge(consts_ready, CONSTS + 1)
            iteration(batch(0, 1), False, 2)
            iteration(batch(0, 2), False, 2)
            with pe.Fori(0, (B - 6) // 2) as i:
                iteration(batch(i, 3), False, 2)
                iteration(batch(i, 4), False, 2)
            for c in range(B - 3, B):
                iteration(batch(0, c), False, B - 1 - c)
            last = batch(0, B - 1)
            pv_mm(last, UNITS - 1)
            out_turn(last, (x_done, B - 1))
            concat_turn(last)
            out_proj(last)


CAPACITY = int(1.25 * B * S / 8)
GROUP = 2
SPLIT_LAG = 2
LAG = 3
Y_AT = LAG + 1


def ffn_phase(nc, name, x, ident, w, kind, gate, scratch):
    E = {"capacity": 8, "groups": 32, "first": 8}[kind]
    shared = {"capacity": 8, "groups": 1, "first": 0}[kind]
    routed = {"capacity": 32, "groups": 16, "first": 22}[kind]
    C = shared + routed
    NW = {"capacity": 8, "groups": 16, "first": 22}[kind]
    with ExitStack() as ctx:
        m = Memory(nc, ctx, name)
        sb, ps, sem = m.sb, m.ps, m.sem
        wg_lo, wg_hi = sb("wg_lo", [D, C, D], F32R), sb("wg_hi", [D, C, D], F32R)
        wu_lo, wu_hi = sb("wu_lo", [D, C, D], F32R), sb("wu_hi", [D, C, D], F32R)
        whole = sb("whole", [D, 2, 3, GROUP, D])
        wd_lo, wd_hi = sb("wd_lo", [D, C, D], F32R), sb("wd_hi", [D, C, D], F32R)
        router = sb("router", [D, E])
        before_ = sb("before", [S, S])
        lower = sb("lower", [S, 8, 8])
        rev = sb("rev", [S, E])
        PARTS = [(c, min(C, c + GROUP)) for c in range(0, C, GROUP)]
        loads = [(router[:, :], w["router"]),
                 (before_[:, :], w["before"]), (lower[:, :, :], w["lower"].partition_broadcast(S)),
                 (rev[:, :], w["rev"][0:E].partition_broadcast(S))]
        biased = kind == "groups"
        if biased:
            bg = sb("bg", [D, C])
            bu = sb("bu", [D, C])
            bd = sb("bd", [E, D])
            bshared = sb("bshared", [D, 1])
            brouter = sb("brouter", [S, E])
            loads += [(bg[:, :], w["bg"]), (bu[:, :], w["bu"]), (bd[:, :], w["bd"]), (bshared[:, :], w["bshared"]),
                      (brouter[:, :], w["brouter"].partition_broadcast(S))]
        LOADED = 16 * len(loads)
        st = sb("stats", [S, B, 6])
        mean = sb("mean", [S, B])
        rstd = sb("rstd", [S, B])
        rms = sb("rms", [S, B])
        tmp = sb("tmp", [S, 4, B])
        xn = sb("xn", [S, BLK, D])
        xT = sb("xT", [D, TOK])
        xh, xl = sb("xh", [D, 2, TOK], F32R), sb("xl", [D, 2, TOK], F32R)
        prob = sb("prob", [S, BLK, E])
        expo = sb("expo", [S, BLK, E])
        masked = sb("masked", [S, BLK, E])
        hit = sb("hit", [S, BLK, E])
        key = sb("key", [S, BLK, E])
        chosen = sb("chosen", [S, BLK, E])
        weight = sb("weight", [S, BLK, E])
        col = sb("col", [S, 8, BLK])
        duel = sb("duel", [S, BLK, 8, 8])
        tie = sb("tie", [S, BLK, 8, 8])
        rank = sb("rank", [S, BLK, 8])
        pairs = sb("pairs", [S, BLK * 8, 6])
        group = sb("group", [S, BLK, 8])
        seen = sb("seen", [S, BLK + 1, 8])
        ones = sb("ones", [S, S])
        wT = sb("wT", [E, 2, TOK])
        wb = sb("wb", [D, 2, NW, TOK])
        NH = 4
        gs = sb("gs", [D, 2, TOK])
        hb = sb("hb", [D, NH + C % 2, TOK])
        hh, hl = sb("hh", [D, 2, TOK], F32R), sb("hl", [D, 2, TOK], F32R)
        yT = sb("yT", [D, TOK])
        p_g = [ps(f"g{i}", [D, 512]) for i in range(2)]
        p_u = [ps(f"u{i}", [D, 512]) for i in range(2)]
        p_y = ps("y", [D, 512])
        p_t = ps("t", [D, 512])
        p_r = ps("r", [D, 512])
        p_w = ps("w", [D, 512])

        passed = sem("passed_sp")
        weights_in = sem("weights_in")
        part_in = [sem(f"part_in{i}") for i in range(2)]
        rounded, w_split, xh_ready, xl_ready = sem("rounded"), sem("w_split"), sem("xh_ready"), sem("xl_ready")
        dve_step = sem("dve_step")
        var_ready, root_ready = sem("var_ready"), sem("root_ready")
        xn_ready, xn_turned, xT_ready = sem("xn_ready"), sem("xn_turned"), sem("xT_ready")
        logits_ready, shifted_ready, expo_ready = sem("logits_ready"), sem("shifted_ready"), sem("expo_ready")
        chosen_ready, place_ready, weight_ready = sem("chosen_ready"), sem("place_ready"), sem("weight_ready")
        w_turned, wT_ready, wT_out, wb_in = sem("w_turned"), sem("wT_ready"), sem("wT_out"), sem("wb_in")
        gu_ready, silu_ready, h_ready, hw_ready, down_done = (sem("gu_ready"), sem("silu_ready"), sem("h_ready"),
                                                             sem("hw_ready"), sem("down_done"))
        hh_ready, hl_ready = sem("hh_ready"), sem("hl_ready")
        yT_ready, y_turned, x_done = sem("yT_ready"), sem("y_turned"), sem("x_done")
        block = ctx.enter_context(nc.Block())
        AT = {"capacity": {"dve": (2, 6, 8, 18), "pe": (3, 5, 16, 20), "act": (4, 7, 21)},
              "groups": {"dve": (0, 3, 4, 6, 8, 9, 10, 11, 12), "pe": (1, 2, None, 13), "act": (1, 4, 14)},
              "first": {"dve": (2, 6, None, None), "pe": (3, 5, None, 9), "act": (4, None, 10)}}[kind]

        def slot(n, c):
            if C % 2:
                return NH if c == C - 1 else c % NH
            return (C * par(n) + c) % NH

        def half(n, c):
            return (C * par(n) + c) % 2

        def earlier(n, c, lag):
            return (n, c - lag) if c >= lag else (nxt(n, -1), C + c - lag)

        def all_blocks(eng, prologue, iteration):
            prologue(batch(0, 0))
            iteration(batch(0, 0), True)
            iteration(batch(0, 1), True)
            with eng.Fori(0, (NBLK - 4) // 2) as i:
                iteration(batch(i, 2), True)
                iteration(batch(i, 3), True)
            iteration(batch(0, NBLK - 2), True)
            iteration(batch(0, NBLK - 1), False)

        if kind == "capacity":
            spreads = [(0, D, 0, NW, None)]
        elif kind == "groups":
            spreads = [(64 * two, 64 * two + 64, 0, NW, two) for two in range(2)]
        else:
            I = 352
            spreads = []
            for e in range(E):
                at, end = I * e, I * (e + 1)
                while at < end:
                    c, r = divmod(at, D)
                    if r == 0 and (end - at) >= D:
                        n = (end - at) // D
                        spreads.append((0, D, c, c + n, e))
                        at += n * D
                    else:
                        n = min(D - r, end - at)
                        spreads.append((r, r + n, c, c + 1, e))
                        at += n
        WB = 16 * len(spreads)

        @block.sync
        def _(sp):
            for dst, src in loads:
                sp.dma_start(dst, src).then_inc(weights_in, 16)
            def part_load(p):
                c0, c1 = PARTS[p]
                if needed(3 * (p - 1)):
                    sp.wait_ge(w_split, 3 * (p - 1))
                for k, key_ in enumerate(("wg", "wu", "wd")):
                    sp.dma_start(whole[:, p % 2, k, 0:c1 - c0, :], w[key_][:, c0:c1, :]).then_inc(part_in[p % 2], 16)

            part_load(0)
            part_load(1)

            def weights_spread(n):
                sp.wait_ge(wT_ready, num(n) + 1)
                sp.dma_start(scratch[par(n)][0:E, :], wT[:, par(n), :]).then_inc(wT_out, 16)
                sp.wait_ge(wT_out, 16 * (num(n) + 1))
                apart(sp, passed)
                if needed(routed * (num(n) - 1)):
                    sp.wait_ge(hw_ready, routed * (num(n) - 1))
                src = scratch[par(n)]
                q = par(n)
                for r0, r1, c0, c1, e in spreads:
                    if kind == "capacity":
                        s_ = src[0:E, :]
                    elif kind == "groups":
                        s_ = src[0:E, :].rearrange("(c two) t -> two c t", two=2)[e]
                    else:
                        s_ = bc(src[e, :], 0, c1 - c0)
                    sp.dma_start(wb[r0:r1, q, c0:c1, :], s_.partition_broadcast(r1 - r0)).then_inc(wb_in, 16)

            def iteration(n, more):
                if opening(n):
                    for p in range(2, len(PARTS)):
                        part_load(p)
                if more:
                    weights_spread(nxt(n, 1))

            all_blocks(sp, weights_spread, iteration)

        @block.gpsimd
        def _(pool):
            def weigh(n, c):
                r = c - shared
                pool.wait_ge(h_ready, C * num(n) + c + 1)
                if r == 0:
                    pool.wait_ge(wb_in, WB * (num(n) + 1))
                q = par(n)
                row = {"capacity": r // 4, "groups": r, "first": r}[kind]
                pool.tensor_tensor(hb[:, slot(n, c), :], hb[:, slot(n, c), :], wb[:, q, row, :], ALU.mult).then_inc(hw_ready, 1)

            def iteration(n, more):
                for c in range(shared, C):
                    weigh(n, c)

            all_blocks(pool, lambda n: None, iteration)

        @block.scalar
        def _(act):
            act.wait_ge(var_ready, 1)
            act.activation(tmp[:, 3, :], tmp[:, 0, :], ACT.Sqrt).then_inc(root_ready, 1)
            if kind == "capacity":
                act.wait_ge(var_ready, 2)
                act.activation(tmp[:, 3, :], tmp[:, 0, :], ACT.Sqrt).then_inc(root_ready, 1)
            act.wait_ge(weights_in, LOADED)

            def prepare(n, part):
                if part == 0:
                    act.wait_ge(xn_turned, num(n) + 1)
                    if needed(C * (num(n) - 1)):
                        act.wait_ge(gu_ready, C * (num(n) - 1))
                    if needed(num(n)):
                        act.wait_ge(logits_ready, num(n))
                        act.wait_ge(xl_ready, num(n))
                    act.activation(xT[:, :], p_t[:, 0:TOK], ACT.Copy).then_inc(xT_ready, 1)
                    act.activation(xh[:, par(n), :], p_t[:, 0:TOK], ACT.Copy).then_inc(xh_ready, 1)
                if part == 1 and kind != "first":
                    act.wait_ge(shifted_ready, num(n) + 1)
                    act.activation(expo[:, :, :], prob[:, :, :], ACT.Exp).then_inc(expo_ready, 1)
                if part == 2:
                    act.wait_ge(w_turned, num(n) + 1)
                    if needed(16 * (num(n) - 1)):
                        act.wait_ge(wT_out, 16 * (num(n) - 1))
                    act.activation(wT[:, par(n), :], p_w[0:E, 0:TOK], ACT.Copy).then_inc(wT_ready, 1)

            def round_weights(p):
                act.wait_ge(part_in[p % 2], 48 * (p // 2 + 1))
                c0, c1 = PARTS[p]
                act.activation(wg_hi[:, c0:c1, :], whole[:, p % 2, 0, 0:c1 - c0, :], ACT.Copy).then_inc(rounded, 1)
                act.activation(wu_hi[:, c0:c1, :], whole[:, p % 2, 1, 0:c1 - c0, :], ACT.Copy).then_inc(rounded, 1)
                act.activation(wd_hi[:, c0:c1, :], whole[:, p % 2, 2, 0:c1 - c0, :], ACT.Copy).then_inc(rounded, 1)

            def round_hidden(n, c):
                if c >= shared:
                    act.wait_ge(hw_ready, routed * num(n) + c - shared + 1)
                else:
                    act.wait_ge(h_ready, C * num(n) + c + 1)
                if needed(C * num(n) + c - 1):
                    act.wait_ge(down_done, C * num(n) + c - 1)
                act.activation(hh[:, half(n, c), :], hb[:, slot(n, c), :], ACT.Copy).then_inc(hh_ready, 1)

            def result(n):
                act.wait_ge(down_done, C * num(n) + C)
                if needed(num(n)):
                    act.wait_ge(y_turned, num(n))
                act.activation(yT[:, :], p_y[:, 0:TOK], ACT.Identity, bias=bshared[:, 0:1] if biased else 0.0).then_inc(yT_ready, 1)

            def silu(n, c):
                act.wait_ge(gu_ready, C * num(n) + c + 1)
                if needed(C * num(n) + (c - 1 if c >= 2 else 0)):
                    act.wait_ge(h_ready, C * num(n) + (c - 1 if c >= 2 else 0))
                act.activation(gs[:, c % 2, :], p_g[c % 2][:, 0:TOK], ACT.Silu,
                               bias=bg[:, c:c + 1] if biased else 0.0).then_inc(silu_ready, 1)

            def iteration(n, more):
                for c in range(C):
                    if more:
                        if c in AT["act"]:
                            prepare(nxt(n, 1), AT["act"].index(c))
                    if opening(n) and c % GROUP == 0 and c // GROUP + 1 < len(PARTS):
                        round_weights(c // GROUP + 1)
                    if c >= SPLIT_LAG or not opening(n):
                        round_hidden(*earlier(n, c, SPLIT_LAG))
                    if c == LAG and not opening(n):
                        result(nxt(n, -1))
                    silu(n, c)
                if not more:
                    for c in range(C - SPLIT_LAG, C):
                        round_hidden(n, c)
                    result(n)

            def prologue(n):
                for part in range(3):
                    prepare(n, part)
                    if part == 0:
                        round_weights(0)

            all_blocks(act, prologue, iteration)

        @block.vector
        def _(dve):
            steps = {"at": 0, "loop": 0}

            def step(ins):
                steps["at"] += 1
                ins.then_inc(dve_step, 1)
                dve.wait_ge(dve_step, steps["loop"] + steps["at"])

            with dve.Fori(0, B) as b:
                nc.vector.bn_stats(st[:, b, :], x[:, b, :]).then_inc(dve_step, 1)
            steps["at"] += B
            dve.wait_ge(dve_step, B)
            rstd_steps(nc, dve, step, st, mean[:, :], rstd[:, :], tmp, var_ready, root_ready, 1e-5)
            if kind == "capacity":
                eps = 1.1920929e-07
                t, v = tmp[:, 1, :], tmp[:, 0, :]
                step(nc.vector.tensor_scalar(t, v, -1e-5, None, ALU.add))
                step(nc.vector.tensor_tensor(t, t, rstd[:, :], ALU.mult))
                step(nc.vector.tensor_tensor(t, t, rstd[:, :], ALU.mult))
                nc.vector.tensor_scalar(v, t, eps, None, ALU.add).then_inc(var_ready, 1)
                dve.wait_ge(root_ready, 2)
                step(nc.vector.reciprocal(rms[:, :], tmp[:, 3, :]))
                step(nc.vector.tensor_tensor(t, rms[:, :], rms[:, :], ALU.mult))
                step(nc.vector.tensor_tensor(t, t, v, ALU.mult))
                step(nc.vector.tensor_scalar(t, t, -0.5, 1.5, ALU.mult, ALU.add))
                step(nc.vector.tensor_tensor(rms[:, :], rms[:, :], t, ALU.mult))
                step(nc.vector.memset(seen[:, :, :], 0.0))
            step(nc.vector.memset(ones[:, :], 1.0))
            dve.wait_ge(weights_in, LOADED)

            def ranks(v, k, out_):
                mine, others = bc(v, 3, 8), bc(v, 2, 8)
                step(nc.vector.tensor_tensor(duel[:, :, :, :], others, mine, ALU.is_gt))
                step(nc.vector.tensor_tensor(tie[:, :, :, :], others, mine, ALU.is_equal))
                step(nc.vector.tensor_tensor(tie[:, :, :, :], tie[:, :, :, :], bc(lower[:, :, :], 1, BLK), ALU.mult))
                step(nc.vector.tensor_tensor(duel[:, :, :, :], duel[:, :, :, :], tie[:, :, :, :], ALU.add))
                step(nc.vector.tensor_reduce(rank[:, :, :], duel[:, :, :, :], AX.X, ALU.add))
                step(nc.vector.tensor_scalar(out_, rank[:, :, :], float(k), None, ALU.is_lt))

            def best(v, out_):
                step(nc.vector.tensor_reduce(col[:, 4, :], v, AX.X, ALU.max))
                step(nc.vector.tensor_tensor(hit[:, :, :], v, bc(col[:, 4, :], 2, E), ALU.is_equal))
                step(nc.vector.tensor_tensor(key[:, :, :], hit[:, :, :], bc(rev[:, :], 1, BLK), ALU.mult))
                step(nc.vector.tensor_reduce(col[:, 5, :], key[:, :, :], AX.X, ALU.max))
                step(nc.vector.tensor_tensor(out_, key[:, :, :], bc(col[:, 5, :], 2, E), ALU.is_equal))

            def prepare(n, part):
                if part == 0:
                    if needed(num(n)):
                        dve.wait_ge(xn_turned, num(n))
                    for j in range(BLK):
                        b = num(n) * BLK + j
                        ins = nc.vector.tensor_scalar(xn[:, j, :], x[:, b, :], mean[:, bass.ds(b, 1)],
                                                      rstd[:, bass.ds(b, 1)], ALU.subtract, ALU.mult)
                        ins.then_inc(xn_ready, 1)
                if part == 1:
                    x_low(n)
                logits = p_r[0:S, 0:BLK * E].rearrange("p (b e) -> p b e", b=BLK)
                if part == 1:
                    dve.wait_ge(logits_ready, num(n) + 1)
                    if needed(num(n)):
                        dve.wait_ge(w_turned, num(n))
                    if kind == "first":
                        step(nc.vector.tensor_copy(prob[:, :, :], logits))
                        best(prob[:, :, :], chosen[:, :, :])
                        nc.vector.tensor_copy(weight[:, :, :], chosen[:, :, :]).then_inc(weight_ready, 1)
                        return
                    if kind == "capacity":
                        step(nc.vector.tensor_tensor(prob[:, :, :], logits, bc(rms[:, bass.ds(num(n) * BLK, BLK)], 2, E), ALU.mult))
                    else:
                        step(nc.vector.tensor_tensor(prob[:, :, :], logits, bc(brouter[:, :], 1, BLK), ALU.add))
                    step(nc.vector.tensor_reduce(col[:, 0, :], prob[:, :, :], AX.X, ALU.max))
                    nc.vector.tensor_tensor(prob[:, :, :], prob[:, :, :], bc(col[:, 0, :], 2, E),
                                            ALU.subtract).then_inc(shifted_ready, 1)
                if part == 2 and kind != "first":
                    dve.wait_ge(expo_ready, num(n) + 1)
                    step(nc.vector.tensor_reduce(col[:, 1, :], expo[:, :, :], AX.X, ALU.add))
                    step(nc.vector.reciprocal(col[:, 2, :], col[:, 1, :]))
                    step(nc.vector.tensor_tensor(prob[:, :, :], expo[:, :, :], bc(col[:, 2, :], 2, E), ALU.mult))
                    if kind == "capacity":
                        ranks(prob[:, :, :], 2, chosen[:, :, :])
                        step(nc.vector.tensor_copy(seen[:, 0, :], seen[:, BLK, :]))
                        for j in range(BLK):
                            ins = nc.vector.tensor_tensor(seen[:, j + 1, :], seen[:, j, :], chosen[:, j, :], ALU.add)
                            if j < BLK - 1:
                                step(ins)
                            else:
                                ins.then_inc(chosen_ready, 1)
                        step(nc.vector.tensor_tensor(masked[:, :, :], prob[:, :, :], chosen[:, :, :], ALU.mult))
                        step(nc.vector.tensor_reduce(col[:, 1, :], masked[:, :, :], AX.X, ALU.add))
                        step(nc.vector.reciprocal(col[:, 2, :], col[:, 1, :]))
                        step(nc.vector.tensor_tensor(masked[:, :, :], masked[:, :, :], bc(col[:, 2, :], 2, E), ALU.mult))
                    else:
                        p4 = prob[:, :, :].rearrange("p b (g k) -> p (b g) k", k=4)
                        for a, (i, j) in enumerate([(0, 1), (0, 2), (0, 3), (1, 2), (1, 3), (2, 3)]):
                            step(nc.vector.tensor_tensor(pairs[:, :, a], p4[:, :, i], p4[:, :, j], ALU.add))
                        step(nc.vector.tensor_reduce(group[:, :, :].rearrange("p b g -> p (b g)"), pairs[:, :, :], AX.X, ALU.max))
                if kind == "groups" and part >= 3:
                    p4 = prob[:, :, :].rearrange("p b (g k) -> p (b g) k", k=4)
                    if part == 3:
                        ranks(group[:, :, :], 4, group[:, :, :])
                    if part == 4:
                        kept = bc(group[:, :, :].rearrange("p b g -> p (b g)"), 2, 4)
                        m4 = masked[:, :, :].rearrange("p b (g k) -> p (b g) k", k=4)
                        h4 = hit[:, :, :].rearrange("p b (g k) -> p (b g) k", k=4)
                        step(nc.vector.tensor_tensor(m4, p4, kept, ALU.mult))
                        step(nc.vector.tensor_scalar(h4, kept, -1.0, None, ALU.add))
                        step(nc.vector.tensor_tensor(masked[:, :, :], masked[:, :, :], hit[:, :, :], ALU.add))
                    if part >= 5:
                        r = part - 5
                        now = chosen if r == 0 else hit
                        best(masked[:, :, :], now[:, :, :])
                        if r > 0:
                            step(nc.vector.tensor_tensor(chosen[:, :, :], chosen[:, :, :], hit[:, :, :], ALU.add))
                        if r < 3:
                            step(nc.vector.scalar_tensor_tensor(masked[:, :, :], now[:, :, :], -4.0, masked[:, :, :],
                                                                ALU.mult, ALU.add))
                    if part == 8:
                        nc.vector.tensor_tensor(weight[:, :, :], prob[:, :, :], chosen[:, :, :], ALU.mult).then_inc(weight_ready, 1)
                if part == 3 and kind == "capacity":
                    dve.wait_ge(place_ready, num(n) + 1)
                    place = p_r[0:S, 256:256 + BLK * E].rearrange("p (b e) -> p b e", b=BLK)
                    step(nc.vector.tensor_scalar(hit[:, :, :], place, float(CAPACITY), None, ALU.is_lt))
                    nc.vector.tensor_tensor(weight[:, :, :], masked[:, :, :], hit[:, :, :], ALU.mult).then_inc(weight_ready, 1)

            def split_weights(p):
                c0, c1 = PARTS[p]
                for k, (low, upper) in enumerate(((wg_lo, wg_hi), (wu_lo, wu_hi), (wd_lo, wd_hi))):
                    dve.wait_ge(rounded, 3 * p + k + 1)
                    nc.vector.tensor_tensor(low[:, c0:c1, :], whole[:, p % 2, k, 0:c1 - c0, :],
                                            upper[:, c0:c1, :].bitcast(F32), ALU.subtract).then_inc(w_split, 1)

            def x_low(n):
                dve.wait_ge(xh_ready, num(n) + 1)
                nc.vector.tensor_tensor(xl[:, par(n), :], xT[:, :], xh[:, par(n), :].bitcast(F32),
                                        ALU.subtract).then_inc(xl_ready, 1)

            def hidden(n, c):
                dve.wait_ge(silu_ready, C * num(n) + c + 1)
                if needed(C * num(n) + c - NH + 1):
                    dve.wait_ge(hl_ready, C * num(n) + c - NH + 1)
                if biased:
                    nc.vector.scalar_tensor_tensor(hb[:, slot(n, c), :], p_u[c % 2][:, 0:TOK], bu[:, c:c + 1], gs[:, c % 2, :],
                                                   ALU.add, ALU.mult).then_inc(h_ready, 1)
                else:
                    nc.vector.tensor_tensor(hb[:, slot(n, c), :], p_u[c % 2][:, 0:TOK], gs[:, c % 2, :],
                                            ALU.mult).then_inc(h_ready, 1)

            def hidden_low(n, c):
                dve.wait_ge(hh_ready, C * num(n) + c + 1)
                nc.vector.tensor_tensor(hl[:, half(n, c), :], hb[:, slot(n, c), :], hh[:, half(n, c), :].bitcast(F32),
                                        ALU.subtract).then_inc(hl_ready, 1)

            def update_x(n):
                dve.wait_ge(y_turned, num(n) + 1)
                at = x[:, :, :].rearrange("p b d -> p (b d)")[:, bass.ds(num(n) * BLK * D, BLK * D)]
                nc.vector.scalar_tensor_tensor(at, p_w[0:S, :], gate, at, ALU.mult, ALU.add).then_inc(x_done, 1)

            def iteration(n, more):
                for c in range(C):
                    if more and c in AT["dve"]:
                        prepare(nxt(n, 1), AT["dve"].index(c))
                    if opening(n) and c % GROUP == 0 and c // GROUP + 1 < len(PARTS):
                        split_weights(c // GROUP + 1)
                    if c >= SPLIT_LAG or not opening(n):
                        hidden_low(*earlier(n, c, SPLIT_LAG))
                    hidden(n, c)
                    if c == Y_AT and not opening(n):
                        update_x(nxt(n, -1))
                if not more:
                    for c in range(C - SPLIT_LAG, C):
                        hidden_low(n, c)
                    update_x(n)

            for part in range(len(AT["dve"])):
                prepare(batch(0, 0), part)
            split_weights(0)
            start = steps["at"]
            per = {"capacity": 2 + 3 + 6 + 1 + 3 + 4 + 1, "groups": 2 + 3 + 6 + 1 + 6 + 3 + 20 + 3 + 3, "first": 6}[kind]
            iteration(batch(0, 0), True)
            iteration(batch(0, 1), True)
            start = steps["at"]
            with dve.Fori(0, (NBLK - 4) // 2) as i:
                steps["loop"] = i * (2 * per)
                iteration(batch(i, 2), True)
                iteration(batch(i, 3), True)
                assert steps["at"] == start + 2 * per, (steps["at"] - start, per)
            steps["loop"] = ((NBLK - 4) // 2 - 1) * 2 * per
            iteration(batch(0, NBLK - 2), True)
            iteration(batch(0, NBLK - 1), False)

        @block.tensor
        def _(pe):
            pe.wait_ge(weights_in, LOADED)

            def prepare(n, part):
                if part == 0:
                    for j in range(BLK):
                        pe.wait_ge(xn_ready, BLK * num(n) + j + 1)
                        ins = pe.transpose(p_t[:, j * S:(j + 1) * S], xn[:, j, :], ident[0:S, 0:S])
                    ins.then_inc(xn_turned, 1)
                if part == 1:
                    pe.wait_ge(xT_ready, num(n) + 1)
                    if needed(num(n)):
                        pe.wait_ge(weight_ready, num(n))
                    for j in range(BLK):
                        ins = pe.matmul(p_r[0:S, j * E:(j + 1) * E], xT[:, j * S:(j + 1) * S], router[:, :],
                                        start=True, stop=True)
                    ins.then_inc(logits_ready, 1)
                if part == 2 and kind == "capacity":
                    pe.wait_ge(chosen_ready, num(n) + 1)
                    place = p_r[0:S, 256:256 + BLK * E]
                    pe.matmul(place, before_[:, :], chosen[:, :, :].rearrange("p b e -> p (b e)"), start=True, stop=False)
                    pe.matmul(place, ones[:, :], seen[:, 0:BLK, :].rearrange("p b e -> p (b e)"), start=False,
                              stop=True).then_inc(place_ready, 1)
                if part == 3:
                    pe.wait_ge(weight_ready, num(n) + 1)
                    if needed(num(n)):
                        pe.wait_ge(wT_ready, num(n))
                    if needed(num(n) - 1):
                        pe.wait_ge(x_done, num(n) - 1)
                    for j in range(BLK):
                        ins = pe.transpose(p_w[0:E, j * S:(j + 1) * S], weight[:, j, :], ident[0:S, 0:S])
                    ins.then_inc(w_turned, 1)

            def product(out_, hi, lo, upper, lower_, start=True, stop=True):
                pe.matmul(out_, lo, upper, start=start, stop=False)
                pe.matmul(out_, hi, lower_, start=False, stop=False)
                return pe.matmul(out_, hi, upper, start=False, stop=stop)

            def gate_up(n, c):
                if c == 0:
                    pe.wait_ge(xl_ready, num(n) + 1)
                if opening(n) and c % GROUP == 0:
                    pe.wait_ge(w_split, 3 * (c // GROUP) + 3)
                before = C * num(n) + (c - 1 if c >= 2 else 0)
                if needed(before):
                    pe.wait_ge(silu_ready, before)
                product(p_g[c % 2][:, 0:TOK], wg_hi[:, c, :], wg_lo[:, c, :], xh[:, par(n), :], xl[:, par(n), :])
                if needed(before):
                    pe.wait_ge(h_ready, before)
                product(p_u[c % 2][:, 0:TOK], wu_hi[:, c, :], wu_lo[:, c, :], xh[:, par(n), :], xl[:, par(n), :]).then_inc(gu_ready, 1)

            def down(n, c):
                if c == 0:
                    if needed(num(n)):
                        pe.wait_ge(yT_ready, num(n))
                if c == 1 and biased:
                    pe.matmul(p_y[:, 0:TOK], bd[:, :], wT[:, par(n), :], start=False, stop=False)
                pe.wait_ge(hl_ready, C * num(n) + c + 1)
                product(p_y[:, 0:TOK], wd_hi[:, c, :], wd_lo[:, c, :], hh[:, half(n, c), :], hl[:, half(n, c), :],
                        start=(c == 0), stop=(c == C - 1)).then_inc(down_done, 1)

            def y_turn(n, last):
                pe.wait_ge(yT_ready, num(n) + 1)
                pe.wait_ge(wT_ready, num(n) + (1 if last else 2))
                for j in range(BLK):
                    ins = pe.transpose(p_w[0:S, j * D:(j + 1) * D], yT[:, j * S:(j + 1) * S], ident[:, :])
                ins.then_inc(y_turned, 1)

            def iteration(n, more):
                for c in range(C):
                    if c == Y_AT and not opening(n):
                        y_turn(nxt(n, -1), False)
                    if more and c in AT["pe"]:
                        prepare(nxt(n, 1), AT["pe"].index(c))
                    gate_up(n, c)
                    if c >= LAG or not opening(n):
                        down(*earlier(n, c, LAG))
                if not more:
                    for c in range(C - LAG, C):
                        down(n, c)
                    y_turn(n, True)

            def prologue(n):
                for part in range(4):
                    prepare(n, part)

            all_blocks(pe, prologue, iteration)


def wide_attention_phase(nc, name, x, xnT, ident, w, dram, gate):
    SCALE = D ** -0.5
    with ExitStack() as ctx:
        m = Memory(nc, ctx, name)
        sb, ps, sem = m.sb, m.ps, m.sem
        wq, wkT, wv = sb("wq", [D, D]), sb("wkT", [D, D]), sb("wv", [D, D])
        bq, bk, bv = sb("bq", [D, 1]), sb("bk", [D, 1]), sb("bv", [S, D])
        gamma, beta = sb("gamma", [S, D]), sb("beta", [S, D])
        loads = [(wq[:, :], w["wq"]), (wkT[:, :], w["wkT"]), (wv[:, :], w["wv"]), (bq[:, :], w["bq"]), (bk[:, :], w["bk"]),
                 (bv[:, :], w["bv"].partition_broadcast(S)), (gamma[:, :], w["gamma"].partition_broadcast(S)),
                 (beta[:, :], w["beta"].partition_broadcast(S))]
        LOADED = 16 * len(loads)
        ctxT = sb("ctxT", [D, 2, KEYS])
        ctxn = sb("ctxn", [D, 2, KT, D])
        mask_i = sb("mask_i", [S, 2, KEYS], I32)
        pen = sb("pen", [S, 2, KEYS])
        sc = sb("sc", [S, 2, KEYS])
        probs = sb("probs", [S, 2, KEYS])
        probsT = sb("probsT", [D, 3, 4 * S])
        qT = sb("qT", [D, S])
        qk = sb("qk", [D, 2, S])
        qbk = sb("qbk", [S, 2])
        mx = sb("mx", [S, 2, NCH])
        top = sb("top", [S, 2])
        shift = sb("shift", [S, 2])
        rs = sb("rs", [S, 2])
        rrs = sb("rrs", [S, 2])
        oT = sb("oT", [D, S])
        con = sb("con", [S, B, D])
        st = sb("stats", [S, B, 6])
        mean, rstd, tmp = sb("mean", [S, B]), sb("rstd", [S, B]), sb("tmp", [S, 4, B])
        p_s = [ps(f"scores{i}", [S, 512]) for i in range(NCH)]
        p_t = [ps(f"turned{i}", [D, 512]) for i in range(2)]
        p_o = ps("weighted", [D, 512])
        p_q = ps("q", [D, 512])
        p_c = ps("context", [S, 512])

        passed = {e: sem("passed_" + e) for e in ("pool", "dve")}
        weights_in = sem("weights_in")
        ctxT_in = [sem(f"ctxT_in{i}") for i in range(2)]
        ctxn_in = [sem(f"ctxn_in{i}") for i in range(2)]
        mask_in = [sem(f"mask_in{i}") for i in range(2)]
        pen_ready = sem("pen_ready")
        q_done, q_ready, qk_done, qk_ready = sem("q_done"), sem("q_ready"), sem("qk_done"), sem("qk_ready")
        scores_done, masked, shift_ready, exp_done = sem("scores_done"), sem("masked"), sem("shift_ready"), sem("exp_done")
        turned, turned_out, pv_done, oT_ready = sem("turned"), sem("turned_out"), sem("pv_done"), sem("oT_ready")
        wv_done, con_ready, dve_step = sem("wv_done"), sem("con_ready"), sem("dve_step")
        var_ready, root_ready = sem("var_ready"), sem("root_ready")
        normed, scaled, shifted = sem("normed"), sem("scaled"), sem("shifted")
        block = ctx.enter_context(nc.Block())
        GT = [min(4, KT - 4 * g) for g in range(3)]

        def all_batches(eng, iteration):
            iteration(batch(0, 0), 2)
            iteration(batch(0, 1), 2)
            iteration(batch(0, 2), 2)
            with eng.Fori(0, (B - 6) // 2) as i:
                iteration(batch(i, 3), 2)
                iteration(batch(i, 4), 2)
            for c in range(B - 3, B):
                iteration(batch(0, c), min(2, B - 1 - c))

        @block.sync
        def _(sp):
            for dst, src in loads:
                sp.dma_start(dst, src).then_inc(weights_in, 16)

            def load(b):
                if needed(num(b) - 1):
                    sp.wait_ge(pen_ready, num(b) - 1)
                sp.dma_start(mask_i[:, par(b), :], dram["mask2"][num(b)]).then_inc(mask_in[par(b)], 16)
                if needed(NCH * (num(b) - 1)):
                    sp.wait_ge(scores_done, NCH * (num(b) - 1))
                sp.dma_start(ctxT[:, par(b), :], dram["ctxT"][num(b)]).then_inc(ctxT_in[par(b)], 16)
                if needed(3 * (num(b) - 1)):
                    sp.wait_ge(pv_done, 3 * (num(b) - 1))
                sp.dma_start(ctxn[:, par(b), 0:KT - 1, :], dram["ctxn"][num(b)][0:(KT - 1) * D, :].rearrange(
                    "(t p) d -> p t d", p=D)).then_inc(ctxn_in[par(b)], 16)
                sp.dma_start(ctxn[0:LAST, par(b), KT - 1, :], dram["ctxn"][num(b)][(KT - 1) * D:KEYS, :]).then_inc(
                    ctxn_in[par(b)], 16)

            load(batch(0, 0))
            load(batch(0, 1))

            def iteration(b, ahead):
                if ahead >= 2:
                    load(nxt(b, 2))

            all_batches(sp, iteration)

        @block.gpsimd
        def _(pool):
            def penalty(b):
                pool.wait_ge(mask_in[par(b)], 16 * (nth(b) + 1))
                if needed(NCH * (num(b) - 1)):
                    pool.wait_ge(masked, NCH * (num(b) - 1))
                apart(pool, passed["pool"])
                pool.tensor_scalar(pen[:, par(b), :], mask_i[:, par(b), :], 0, FAR, ALU.is_equal, ALU.mult).then_inc(pen_ready, 1)

            penalty(batch(0, 0))
            penalty(batch(0, 1))

            def iteration(b, ahead):
                if ahead >= 2:
                    penalty(nxt(b, 2))

            all_batches(pool, iteration)
            for c in range(B // 2, B, BLK):
                pool.wait_ge(normed, c // BLK + 1)
                v = con[:, c:c + BLK, :]
                pool.tensor_tensor(v, v, bc(gamma[:, :], 1, BLK), ALU.mult).then_inc(scaled, 1)
                pool.wait_ge(scaled, c // BLK - B // 2 // BLK + 1)
                pool.tensor_tensor(v, v, bc(beta[:, :], 1, BLK), ALU.add).then_inc(shifted, 1)

        @block.scalar
        def _(act):
            act.wait_ge(weights_in, LOADED)

            def q_out(b):
                act.wait_ge(q_done, num(b) + 1)
                if needed(num(b)):
                    act.wait_ge(qk_done, num(b))
                act.activation(qT[:, :], p_q[:, 0:S], ACT.Identity, bias=bq[:, 0:1]).then_inc(q_ready, 1)

            def qk_out(b):
                act.wait_ge(qk_done, num(b) + 1)
                if needed(NCH * (num(b) - 1)):
                    act.wait_ge(scores_done, NCH * (num(b) - 1))
                act.activation(qk[:, par(b), :], p_q[:, S:2 * S], ACT.Copy)
                if needed(num(b) - 1):
                    act.wait_ge(shift_ready, num(b) - 1)
                act.activation(qbk[:, par(b):par(b) + 1], p_q[0:S, 2 * S:2 * S + 1], ACT.Copy).then_inc(qk_ready, 1)

            def exponential(b):
                act.wait_ge(shift_ready, num(b) + 1)
                if needed(3 * (num(b) - 1)):
                    act.wait_ge(turned, 3 * (num(b) - 1))
                if needed(num(b) - 1):
                    act.wait_ge(con_ready, num(b) - 1)
                act.activation(probs[:, par(b), :], sc[:, par(b), :], ACT.Exp, bias=shift[:, par(b):par(b) + 1], scale=SCALE,
                               accum_out=rs[:, par(b):par(b) + 1]).then_inc(exp_done, 1)

            def turned_copy(b, g):
                act.wait_ge(turned, 3 * num(b) + g + 1)
                if needed(3 * (num(b) - 1) + g + 1):
                    act.wait_ge(pv_done, 3 * (num(b) - 1) + g + 1)
                n = GT[g] * S
                act.activation(probsT[:, g, 0:n], p_t[(par(b) + g) % 2][:, 0:n], ACT.Copy).then_inc(turned_out, 1)

            b0, b1 = batch(0, 0), batch(0, 1)
            q_out(b0)
            qk_out(b0)
            exponential(b0)
            q_out(b1)
            qk_out(b1)

            def iteration(b, ahead):
                turned_copy(b, 0)
                turned_copy(b, 1)
                turned_copy(b, 2)
                if ahead >= 2:
                    q_out(nxt(b, 2))
                if ahead >= 1:
                    exponential(nxt(b, 1))
                if ahead >= 2:
                    qk_out(nxt(b, 2))

            all_batches(act, iteration)
            act.wait_ge(var_ready, 1)
            act.activation(tmp[:, 3, :], tmp[:, 0, :], ACT.Sqrt).then_inc(root_ready, 1)

        @block.vector
        def _(dve):
            steps = {"at": 0, "loop": 0}

            def step(ins):
                steps["at"] += 1
                ins.then_inc(dve_step, 1)
                dve.wait_ge(dve_step, steps["loop"] + steps["at"])

            def mask_scores(b, k):
                o, n = CHUNKS[k]
                if k == 0:
                    dve.wait_ge(pen_ready, num(b) + 1)
                    if needed(num(b) - 1):
                        dve.wait_ge(exp_done, num(b) - 1)
                dve.wait_ge(scores_done, NCH * num(b) + k + 1)
                apart(dve, passed["dve"])
                nc.vector.tensor_tensor_reduce(sc[:, par(b), o:o + n], p_s[k][:, 0:n], pen[:, par(b), o:o + n], 1.0, -3.0e38,
                                               ALU.add, ALU.max, mx[:, par(b), k:k + 1]).then_inc(masked, 1)

            def maximum(b):
                q = slice(par(b), par(b) + 1)
                dve.wait_ge(masked, NCH * num(b) + NCH)
                dve.wait_ge(qk_ready, num(b) + 1)
                step(nc.vector.tensor_reduce(top[:, q], mx[:, par(b), :], AX.X, ALU.max))
                step(nc.vector.tensor_tensor(top[:, q], top[:, q], qbk[:, q], ALU.add))
                step(nc.vector.tensor_tensor(top[:, q], qbk[:, q], top[:, q], ALU.subtract))
                nc.vector.tensor_scalar(shift[:, q], top[:, q], SCALE, None, ALU.mult).then_inc(shift_ready, 1)

            def weighted_copy(b):
                q = slice(par(b), par(b) + 1)
                dve.wait_ge(exp_done, num(b) + 1)
                step(nc.vector.reciprocal(rrs[:, q], rs[:, q]))
                dve.wait_ge(pv_done, 3 * num(b) + 3)
                if needed(num(b)):
                    dve.wait_ge(wv_done, num(b))
                nc.vector.tensor_copy(oT[:, :], p_o[:, 0:S]).then_inc(oT_ready, 1)

            def context_out(b):
                q = slice(par(b), par(b) + 1)
                dve.wait_ge(wv_done, num(b) + 1)
                at = con[:, :, :].rearrange("p b d -> p (b d)")[:, bass.ds(num(b) * D, D)]
                nc.vector.scalar_tensor_tensor(at, p_c[:, 0:D], rrs[:, q], bv[:, :], ALU.mult, ALU.add).then_inc(con_ready, 1)
                dve.wait_ge(con_ready, num(b) + 1)
                nc.vector.bn_stats(st[:, :, :].rearrange("p b s -> p (b s)")[:, bass.ds(num(b) * 6, 6)], at)

            for k in range(NCH):
                mask_scores(batch(0, 0), k)
            maximum(batch(0, 0))
            dve.wait_ge(weights_in, LOADED)

            def iteration(b, ahead, first=False):
                for k in range(NCH):
                    if ahead >= 1:
                        mask_scores(nxt(b, 1), k)
                    if k == 1 and not first:
                        context_out(nxt(b, -1))
                if ahead >= 1:
                    maximum(nxt(b, 1))
                weighted_copy(b)

            iteration(batch(0, 0), 2, first=True)
            iteration(batch(0, 1), 2)
            iteration(batch(0, 2), 2)
            per = 4
            with dve.Fori(0, (B - 6) // 2) as i:
                start = steps["at"]
                steps["loop"] = i * (2 * per)
                iteration(batch(i, 3), 2)
                iteration(batch(i, 4), 2)
                assert steps["at"] == start + 2 * per, (start, steps["at"])
            steps["loop"] = ((B - 6) // 2 - 1) * 2 * per
            for c in range(B - 3, B):
                iteration(batch(0, c), min(2, B - 1 - c))
            context_out(batch(0, B - 1))
            step(nc.vector.memset(shift[:, :], 0.0))
            rstd_steps(nc, dve, step, st, mean[:, :], rstd[:, :], tmp, var_ready, root_ready, 1e-5)
            for j in range(B // BLK):
                c = j * BLK
                for b in range(c, c + BLK):
                    ins = nc.vector.tensor_scalar(con[:, b, :], con[:, b, :], mean[:, b:b + 1], rstd[:, b:b + 1],
                                                  ALU.subtract, ALU.mult)
                ins.then_inc(normed, 1)
            for c in range(0, B, BLK):
                v, r = con[:, c:c + BLK, :], x[:, c:c + BLK, :]
                if c < B // 2:
                    dve.wait_ge(normed, c // BLK + 1)
                    step(nc.vector.tensor_tensor(v, v, bc(gamma[:, :], 1, BLK), ALU.mult))
                    step(nc.vector.tensor_tensor(v, v, bc(beta[:, :], 1, BLK), ALU.add))
                else:
                    dve.wait_ge(shifted, (c - B // 2) // BLK + 1)
                nc.vector.scalar_tensor_tensor(r, v, gate, r, ALU.mult, ALU.add)

        @block.tensor
        def _(pe):
            pe.wait_ge(weights_in, LOADED)

            def q_proj(b):
                if needed(num(b)):
                    pe.wait_ge(qk_ready, num(b))
                pe.matmul(p_q[:, 0:S], wq[:, :], xnT[:, bass.ds(num(b) * S, S)], start=True, stop=True).then_inc(q_done, 1)

            def qk_proj(b):
                pe.wait_ge(q_ready, num(b) + 1)
                pe.matmul(p_q[:, S:2 * S], wkT[:, :], qT[:, :], start=True, stop=True)
                pe.matmul(p_q[0:S, 2 * S:2 * S + 1], qT[:, :], bk[:, :], start=True, stop=True).then_inc(qk_done, 1)

            def scores(b, k):
                o, n = CHUNKS[k]
                if k == 0:
                    pe.wait_ge(qk_ready, num(b) + 1)
                    pe.wait_ge(ctxT_in[par(b)], 16 * (nth(b) + 1))
                if needed(NCH * (num(b) - 1) + k + 1):
                    pe.wait_ge(masked, NCH * (num(b) - 1) + k + 1)
                pe.matmul(p_s[k][:, 0:n], qk[:, par(b), :], ctxT[:, par(b), o:o + n], start=True, stop=True).then_inc(scores_done, 1)

            def turn(b, g):
                pe.wait_ge(exp_done, num(b) + 1)
                if needed(3 * num(b) + g - 1):
                    pe.wait_ge(turned_out, 3 * num(b) + g - 1)
                for t in range(GT[g]):
                    o = (4 * g + t) * D
                    r = min(D, KEYS - o)
                    ins = pe.transpose(p_t[(par(b) + g) % 2][0:r, t * S:(t + 1) * S], probs[:, par(b), o:o + r], ident[0:S, 0:S])
                ins.then_inc(turned, 1)

            def pv(b, g):
                pe.wait_ge(turned_out, 3 * num(b) + g + 1)
                if g == 0:
                    pe.wait_ge(ctxn_in[par(b)], 32 * (nth(b) + 1))
                    if needed(num(b)):
                        pe.wait_ge(oT_ready, num(b))
                for t in range(GT[g]):
                    tile = 4 * g + t
                    r = D if tile < KT - 1 else LAST
                    ins = pe.matmul(p_o[:, 0:S], ctxn[0:r, par(b), tile, :], probsT[0:r, g, t * S:(t + 1) * S],
                                    start=(tile == 0), stop=(tile == KT - 1))
                ins.then_inc(pv_done, 1)

            def values(b):
                pe.wait_ge(oT_ready, num(b) + 1)
                if needed(num(b)):
                    pe.wait_ge(con_ready, num(b))
                pe.matmul(p_c[:, 0:D], oT[:, :], wv[:, :], start=True, stop=True).then_inc(wv_done, 1)

            b0, b1 = batch(0, 0), batch(0, 1)
            q_proj(b0)
            qk_proj(b0)
            for k in range(NCH):
                scores(b0, k)
            q_proj(b1)
            qk_proj(b1)

            def iteration(b, ahead, first=False):
                b1, b2 = nxt(b, 1), nxt(b, 2)
                if ahead >= 1:
                    scores(b1, 0)
                if not first:
                    values(nxt(b, -1))
                turn(b, 0)
                if ahead >= 1:
                    scores(b1, 1)
                turn(b, 1)
                if ahead >= 1:
                    scores(b1, 2)
                pv(b, 0)
                turn(b, 2)
                if ahead >= 2:
                    q_proj(b2)
                pv(b, 1)
                if ahead >= 2:
                    qk_proj(b2)
                pv(b, 2)

            iteration(b0, 2, first=True)
            iteration(batch(0, 1), 2)
            iteration(batch(0, 2), 2)
            with pe.Fori(0, (B - 6) // 2) as i:
                iteration(batch(i, 3), 2)
                iteration(batch(i, 4), 2)
            for c in range(B - 3, B):
                iteration(batch(0, c), min(2, B - 1 - c))
            values(batch(0, B - 1))


def channel_mix_phase(nc, name, x, xnT, ident, w, gate):
    with ExitStack() as ctx:
        m = Memory(nc, ctx, name)
        sb, ps, sem = m.sb, m.ps, m.sem
        wr, wk, wv = sb("wr", [D, D]), sb("wk", [D, D]), sb("wv", [D, D])
        mu = sb("mu", [D, 2])
        loads = [(wr[:, :], w["wr"]), (wk[:, :], w["wk"]), (wv[:, :], w["wv"]), (mu[:, :], w["mu"])]
        rest = sb("rest", [D, 2])
        old = sb("old", [D, 2, 2, BLK, S])
        mix = sb("mix", [D, 2, 2, BLK, S])
        gated = sb("gated", [D, 2, TOK])
        pos = sb("pos", [D, 2, TOK])
        y = sb("y", [D, 2, TOK])
        p_rk = [[ps(f"{n}{i}", [D, 512]) for n in "rk"] for i in range(2)]
        p_v = [ps(f"v{i}", [D, 512]) for i in range(2)]
        p_y = [ps(f"y{i}", [S, 512]) for i in range(2)]
        weights_in = sem("weights_in")
        rest_ready, old_ready, mix_ready = sem("rest_ready"), sem("old_ready"), sem("mix_ready")
        rk_done, gate_ready, pos_ready, act_ready = sem("rk_done"), sem("gate_ready"), sem("pos_ready"), sem("act_ready")
        v_done, y_ready, turned, x_done, zeroed = sem("v_done"), sem("y_ready"), sem("turned"), sem("x_done"), sem("zeroed")
        block = ctx.enter_context(nc.Block())

        def all_blocks(eng, iteration):
            iteration(batch(0, 0), True)
            iteration(batch(0, 1), True)
            iteration(batch(0, 2), True)
            with eng.Fori(0, (NBLK - 4) // 2) as i:
                iteration(batch(i, 3), True)
                iteration(batch(i, 4), True)
            iteration(batch(0, NBLK - 1), False)

        @block.sync
        def _(sp):
            for dst, src in loads:
                sp.dma_start(dst, src).then_inc(weights_in, 16)

        @block.gpsimd
        def _(pool):
            pool.memset(old[:, :, :, :, 0:1], 0.0).then_inc(zeroed, 1)
            pool.wait_ge(weights_in, 16 * len(loads))
            pool.tensor_scalar(rest[:, :], mu[:, :], -1.0, 1.0, ALU.mult, ALU.add).then_inc(rest_ready, 1)

        @block.scalar
        def _(act):
            act.wait_ge(rest_ready, 1)

            def previous(n):
                src = xnT[:, bass.ds(num(n) * TOK, TOK)].rearrange("p (b s) -> p b s", s=S)[:, :, 0:S - 1]
                if needed(2 * (num(n) - 1)):
                    act.wait_ge(mix_ready, 2 * (num(n) - 1))
                for i in range(2):
                    act.activation(old[:, par(n), i, :, 1:S], src, ACT.Copy, scale=rest[:, i:i + 1]).then_inc(old_ready, 1)

            def activate(n):
                act.wait_ge(rk_done, 2 * num(n) + 1)
                if needed(num(n) - 1):
                    act.wait_ge(y_ready, num(n) - 1)
                act.activation(gated[:, par(n), :], p_rk[par(n)][0][:, 0:TOK], ACT.Sigmoid).then_inc(gate_ready, 1)
                act.wait_ge(rk_done, 2 * num(n) + 2)
                if needed(num(n) - 1):
                    act.wait_ge(v_done, num(n) - 1)
                act.activation(pos[:, par(n), :], p_rk[par(n)][1][:, 0:TOK], ACT.Relu).then_inc(pos_ready, 1)
                act.wait_ge(pos_ready, num(n) + 1)
                act.activation(pos[:, par(n), :], pos[:, par(n), :], ACT.Square).then_inc(act_ready, 1)

            previous(batch(0, 0))

            def iteration(n, more):
                if more:
                    previous(nxt(n, 1))
                activate(n)

            all_blocks(act, iteration)

        @block.vector
        def _(dve):
            dve.wait_ge(weights_in, 16 * len(loads))
            dve.wait_ge(zeroed, 1)

            def mixed(n):
                src = xnT[:, bass.ds(num(n) * TOK, TOK)].rearrange("p (b s) -> p b s", s=S)
                for i in range(2):
                    dve.wait_ge(old_ready, 2 * num(n) + i + 1)
                    if needed(2 * (num(n) - 2) + i + 1):
                        dve.wait_ge(rk_done, 2 * (num(n) - 2) + i + 1)
                    nc.vector.scalar_tensor_tensor(mix[:, par(n), i, :, :], src, mu[:, i:i + 1], old[:, par(n), i, :, :],
                                                   ALU.mult, ALU.add).then_inc(mix_ready, 1)

            def product(n):
                dve.wait_ge(gate_ready, num(n) + 1)
                dve.wait_ge(v_done, num(n) + 1)
                if needed(num(n) - 1):
                    dve.wait_ge(turned, num(n) - 1)
                nc.vector.tensor_tensor(y[:, par(n), :], p_v[par(n)][:, 0:TOK], gated[:, par(n), :], ALU.mult).then_inc(y_ready, 1)

            def update_x(n):
                dve.wait_ge(turned, num(n) + 1)
                at = x[:, :, :].rearrange("p b d -> p (b d)")[:, bass.ds(num(n) * BLK * D, BLK * D)]
                nc.vector.scalar_tensor_tensor(at, p_y[par(n)][:, :], gate, at, ALU.mult, ALU.add).then_inc(x_done, 1)

            mixed(batch(0, 0))

            def iteration(n, more, first=False):
                if more:
                    mixed(nxt(n, 1))
                product(n)
                if not first:
                    update_x(nxt(n, -1))

            iteration(batch(0, 0), True, first=True)
            iteration(batch(0, 1), True)
            iteration(batch(0, 2), True)
            with dve.Fori(0, (NBLK - 4) // 2) as i:
                iteration(batch(i, 3), True)
                iteration(batch(i, 4), True)
            iteration(batch(0, NBLK - 1), False)
            update_x(batch(0, NBLK - 1))

        @block.tensor
        def _(pe):
            def rk(n):
                for i, wt in enumerate((wr, wk)):
                    pe.wait_ge(mix_ready, 2 * num(n) + i + 1)
                    if needed(num(n) - 1):
                        pe.wait_ge((gate_ready, pos_ready)[i], num(n) - 1)
                    pe.matmul(p_rk[par(n)][i][:, 0:TOK], wt[:, :], mix[:, par(n), i, :, :].rearrange("p b s -> p (b s)"),
                              start=True, stop=True).then_inc(rk_done, 1)

            def value(n):
                pe.wait_ge(act_ready, num(n) + 1)
                if needed(num(n) - 1):
                    pe.wait_ge(y_ready, num(n) - 1)
                pe.matmul(p_v[par(n)][:, 0:TOK], wv[:, :], pos[:, par(n), :], start=True, stop=True).then_inc(v_done, 1)

            def turn(n):
                pe.wait_ge(y_ready, num(n) + 1)
                if needed(num(n) - 1):
                    pe.wait_ge(x_done, num(n) - 1)
                for j in range(BLK):
                    ins = pe.transpose(p_y[par(n)][:, j * D:(j + 1) * D], y[:, par(n), j * S:(j + 1) * S], ident[:, :])
                ins.then_inc(turned, 1)

            pe.wait_ge(weights_in, 16 * len(loads))
            rk(batch(0, 0))

            def iteration(n, more, first=False):
                if more:
                    rk(nxt(n, 1))
                if not first:
                    turn(nxt(n, -1))
                value(n)

            iteration(batch(0, 0), True, first=True)
            iteration(batch(0, 1), True)
            iteration(batch(0, 2), True)
            with pe.Fori(0, (NBLK - 4) // 2) as i:
                iteration(batch(i, 3), True)
                iteration(batch(i, 4), True)
            iteration(batch(0, NBLK - 1), False)
            turn(batch(0, NBLK - 1))


def setup_phase(nc, A, x, ident, gates):
    with ExitStack() as ctx:
        m = Memory(nc, ctx, "setup")
        g = m.sb("g", [D, 8])
        loaded = m.sem("loaded")
        done = m.sem("done")
        block = ctx.enter_context(nc.Block())

        @block.sync
        def _(sp):
            sp.dma_start(x[:, :, :], A["x"]).then_inc(loaded, 16)
            sp.dma_start(ident[:, :], A["ident"]).then_inc(loaded, 16)
            sp.dma_start(g[:, :], A["gates"].partition_broadcast(D)).then_inc(loaded, 16)
            sp.wait_ge(loaded, 48)

        @block.scalar
        def _(act):
            act.wait_ge(loaded, 48)
            nc.scalar.activation(gates[:, :], g[:, :], ACT.Tanh).then_inc(done, 1)


def store_phase(nc, x, out):
    with ExitStack() as ctx:
        stored = ctx.enter_context(nc.semaphore("x_stored"))
        block = ctx.enter_context(nc.Block())

        @block.sync
        def _(sp):
            sp.dma_start(out, x[:, :, :]).then_inc(stored, 16)
            sp.wait_ge(stored, 16)


def flamingo_kernel(nc, A, out):
    with ExitStack() as ctx:
        x = ctx.enter_context(nc.sbuf_tensor("x_res", [S, B, D], F32))
        ident = ctx.enter_context(nc.sbuf_tensor("ident", [D, D], F32))
        gates = ctx.enter_context(nc.sbuf_tensor("gates", [D, 8], F32))
        setup_phase(nc, A, x, ident, gates)
        dram = {"ctxT": A["ctxT"]}
        with nc.sbuf_tensor("xnT_a0", [D, B * S], F32) as xnT:
            layernorm_transposed(nc, "ln_a0", x, xnT, ident)
            w = {k: A["a0_" + k] for k in ("wq", "wk", "wv", "wo", "bq", "bk", "bv", "bo")} | {"blk": A["blk"]}
            attention_phase(nc, "a0", x, xnT, ident, w, dram, DK ** -0.5, gates[0:S, 0:1])
        scratch = [nc.dram_tensor(f"weights_by_token{i}", [32, TOK], F32, kind="Internal").ap() for i in range(2)]

        def ffn(name, kind, layer):
            keys = ("wg", "wu", "wd", "router") + (("bg", "bu", "bd", "bshared", "brouter") if kind == "groups" else ())
            w = {k: A[f"{name}_{k}"] for k in keys} | {k: A[k] for k in ("before", "lower", "rev" + ("32" if kind == "groups" else "8"))}
            w["rev"] = w["rev32" if kind == "groups" else "rev8"]
            ffn_phase(nc, name, x, ident, w, kind, gates[0:S, 4 + layer:5 + layer], scratch)

        ffn("f0", "capacity", 0)
        with nc.sbuf_tensor("xnT_a1", [D, B * S], F32) as xnT:
            layernorm_transposed(nc, "ln_a1", x, xnT, ident)
            w = {k: A["a1_" + k] for k in ("wq", "wk", "wv", "wo")} | {"blk": A["blk"]}
            attention_phase(nc, "a1", x, xnT, ident, w, dram, D ** -0.5, gates[0:S, 1:2], mask=(A["mask1"], A["mask1T"]))
        ffn("f1", "groups", 1)
        with nc.sbuf_tensor("xnT_a2", [D, B * S], F32) as xnT:
            layernorm_transposed(nc, "ln_a2", x, xnT, ident)
            w = {k: A["a2_" + k] for k in ("wq", "wkT", "wv", "bq", "bk", "bv", "gamma", "beta")}
            wide_attention_phase(nc, "a2", x, xnT, ident, w, dram | {"mask2": A["mask2"], "ctxn": A["ctxn"]}, gates[0:S, 2:3])
        ffn("f2", "first", 2)
        with nc.sbuf_tensor("xnT_a3", [D, B * S], F32) as xnT:
            layernorm_transposed(nc, "ln_a3", x, xnT, ident)
            w = {k: A["a3_" + k] for k in ("wq", "wk", "wv", "wo")} | {k: A[k] for k in ("blk", "keyno", "iota")}
            attention_phase(nc, "a3", x, xnT, ident, w, dram, DK ** -0.5, gates[0:S, 3:4], lens=A["lens"])
        with nc.sbuf_tensor("xnT_f3", [D, B * S], F32) as xnT:
            layernorm_transposed(nc, "ln_f3", x, xnT, ident)
            w = {k: A["f3_" + k] for k in ("wr", "wk", "wv", "mu")}
            channel_mix_phase(nc, "f3", x, xnT, ident, w, gates[0:S, 7:8])
        store_phase(nc, x, out)


def host_layout(np, inp):
    f = {k: np.asarray(v) for k, v in inp.items()}
    L = {}
    L["x"] = f["x"].transpose(1, 0, 2)
    L["ident"] = np.eye(D, dtype=np.float32)
    L["gates"] = np.concatenate([f["g_xattn"], f["g_ffn"]])
    L["ctxT"] = f["ctx_1024"].transpose(0, 2, 1)
    rows = np.arange(D)
    L["blk"] = np.concatenate([(rows[:, None] % 32 // DK == np.arange(4)), (rows[:, None] % 16 == np.arange(HEADS))],
                              axis=1).astype(np.float32)

    def parts(w):
        return np.stack([np.concatenate([w[:, 32 * g:32 * g + 32]] * 3, axis=1) for g in range(GROUPS)], axis=1)

    L["a0_wq"], L["a0_wk"], L["a0_wv"], L["a0_wo"] = (parts(f["L0_xattn_Wq"].T), f["L0_xattn_Wk"].T,
                                                     f["L0_xattn_Wv"].T, f["L0_xattn_Wo"].T)
    L["a0_bq"] = np.stack([np.tile(f["L0_xattn_bq"][32 * g:32 * g + 32], 3) for g in range(GROUPS)], axis=1)
    L["a0_bk"], L["a0_bv"], L["a0_bo"] = f["L0_xattn_bk"][:, None], f["L0_xattn_bv"][:, None], f["L0_xattn_bo"][None]
    per_head = np.zeros((D, D), np.float32)
    for n in range(HEADS):
        per_head[DK * n:DK * n + DK, DK * n:DK * n + DK] = f["L1_xattn_W_v"].T
    L["a1_wq"], L["a1_wk"], L["a1_wv"], L["a1_wo"] = parts(per_head), per_head, per_head, f["L1_xattn_W_o"].T
    m1 = f["mask_Bx1xSxS2_ik1"][:, 0]
    L["mask1"] = m1
    m1t = np.zeros((B, KT * D, S), m1.dtype)
    m1t[:, :KEYS] = m1.transpose(0, 2, 1)
    L["mask1T"] = m1t.reshape(B, KT, D, S).transpose(0, 2, 1, 3).reshape(B, D, KT * S)
    L["a3_wq"], L["a3_wk"], L["a3_wv"], L["a3_wo"] = parts(f["L3_xattn_Wq"]), f["L3_xattn_Wk"], f["L3_xattn_Wv"], f["L3_xattn_Wo"]
    L["lens"] = f["mask_B_ik0"]
    L["keyno"] = (np.arange(D)[:, None] + D * np.arange(KT)[None]).astype(np.float32)
    L["iota"] = np.arange(KEYS, dtype=np.float32)
    L["before"] = (np.arange(S)[:, None] < np.arange(S)[None]).astype(np.float32)
    L["lower"] = (np.arange(8)[None] < np.arange(8)[:, None]).astype(np.float32)
    L["rev8"], L["rev32"] = np.arange(8, 0, -1, dtype=np.float32), np.arange(32, 0, -1, dtype=np.float32)

    def first(w):
        return w.reshape(D, -1, D)

    def last(w):
        return w.reshape(-1, D, D).transpose(1, 0, 2)

    def flat(w):
        return w.transpose(1, 0, 2).reshape(D, -1)

    L["f0_wg"] = first(np.concatenate([f["L0_ffn_sg"], flat(f["L0_ffn_rg"])], axis=1))
    L["f0_wu"] = first(np.concatenate([f["L0_ffn_su"], flat(f["L0_ffn_ru"])], axis=1))
    L["f0_wd"] = last(np.concatenate([f["L0_ffn_sd"], f["L0_ffn_rd"].reshape(-1, D)]))
    L["f0_router"] = f["L0_ffn_router_w"].T
    L["f1_wg"] = first(np.concatenate([f["L1_ffn_sw1"], flat(f["L1_ffn_w1"])], axis=1))
    L["f1_wu"] = first(np.concatenate([f["L1_ffn_sw3"], flat(f["L1_ffn_w3"])], axis=1))
    L["f1_wd"] = last(np.concatenate([f["L1_ffn_sw2"], f["L1_ffn_w2"].reshape(-1, D)]))
    L["f1_bg"] = np.concatenate([f["L1_ffn_sb1"], f["L1_ffn_b1"].ravel()]).reshape(-1, D).T
    L["f1_bu"] = np.concatenate([f["L1_ffn_sb3"], f["L1_ffn_b3"].ravel()]).reshape(-1, D).T
    L["f1_bd"], L["f1_bshared"] = f["L1_ffn_b2"], f["L1_ffn_sb2"][:, None]
    L["f1_router"], L["f1_brouter"] = f["L1_ffn_gw"], f["L1_ffn_gb"]
    L["f2_wg"] = first(f["L2_ffn_gate_w"].transpose(2, 0, 1).reshape(D, -1))
    L["f2_wu"] = first(f["L2_ffn_up_w"].transpose(2, 0, 1).reshape(D, -1))
    L["f2_wd"] = last(f["L2_ffn_down_w"].transpose(0, 2, 1).reshape(-1, D))
    L["ctxn"] = f["ctx_1024"]
    L["mask2"] = f["mask_BxSxS2_ik1"]
    L["a2_wq"], L["a2_wkT"], L["a2_wv"] = f["L2_xattn_Wq"], f["L2_xattn_Wk"].T, f["L2_xattn_Wv"]
    L["a2_bq"], L["a2_bk"], L["a2_bv"] = f["L2_xattn_bq"][:, None], f["L2_xattn_bk"][:, None], f["L2_xattn_bv"]
    L["a2_gamma"], L["a2_beta"] = f["L2_xattn_ln_gamma"], f["L2_xattn_ln_beta"]
    L["f3_wr"], L["f3_wk"], L["f3_wv"] = f["L3_ffn_W_r"].T, f["L3_ffn_W_k"].T, f["L3_ffn_W_v"].T
    L["f3_mu"] = np.stack([f["L3_ffn_mu_r"], f["L3_ffn_mu_k"]], axis=1)
    L["f2_router"] = f["L2_ffn_router_w"].T
    return {k: np.ascontiguousarray(v) for k, v in L.items()}


def kernel(**inputs):
    import numpy as _np
    import concourse.bacc as _bacc
    from concourse import mybir as _mybir
    from concourse.bass_utils import run_bass_kernel_spmd as _run

    nc = _bacc.Bacc("TRN2", target_bir_lowering=False, num_devices=1)
    arrays, args = {}, {}
    for name, a in host_layout(_np, inputs).items():
        arrays[f"in_{name}_dram"] = a
        args[name] = nc.dram_tensor(f"in_{name}_dram", a.shape, _mybir.dt.from_np(a.dtype), kind="ExternalInput").ap()
    out = nc.dram_tensor("out_0_dram", (S, B, D), _mybir.dt.float32, kind="ExternalOutput").ap()
    flamingo_kernel(nc, args, out)
    r = _run(nc, [arrays], core_ids=[0])
    return _np.ascontiguousarray(_np.asarray(r.results[0]["out_0_dram"]).transpose(1, 0, 2))
```
